# Optimizing a Trainium2 kernel written in Bass

```python
import numpy as np
import jax
import jax.numpy as jnp

def _softmax(x, axis=-1):
    return jax.nn.softmax(x, axis=axis)

def _gelu(x):
    return jax.nn.gelu(x, approximate=True)

def _silu(x):
    return jax.nn.silu(x)

def _sigmoid(x):
    return jax.nn.sigmoid(x)

def _layernorm(x, axis=-1, eps=1e-05):
    m = jnp.mean(x, axis=axis, keepdims=True)
    v = jnp.var(x, axis=axis, keepdims=True)
    return (x - m) / jnp.sqrt(v + eps)

def _scatter_add(tgt, idx, src, axis=0):
    return tgt.at[idx].add(src)

def _segment_sum(src, seg, n):
    return jax.ops.segment_sum(src, seg, n)
kernel_name = 'mk_adj_resnorm_d2_adj_r2_4facb4'

def setup_inputs(seed: int=0):
    np.random.seed(seed)
    _w = jnp.asarray

    def _rec_inputs():
        import jax
        import jax.numpy as jnp
        _gk = jax.random.key(seed)
        x = -0.0005207 + 1.001 * jax.random.normal(jax.random.fold_in(_gk, 1), (4096, 128), jnp.float32)
        _w = (1.0 + jnp.arange(4096, dtype=jnp.float32)) ** (-0.5)
        _w = _w / _w.mean()
        _pij = jnp.clip(0.000976562 * _w[:, None] * _w[None, :], 0.0, 1.0)
        _a = jax.random.uniform(jax.random.fold_in(_gk, 2), (4096, 4096)) < _pij
        adj = _a.astype(jnp.int32)
        return (x, adj)
    x, adj = _rec_inputs()

    def _L0_gnn_setup():
        import jax, jax.numpy as jnp
        import numpy as np
        N, D = (8192, 128)
        key = jax.random.key(seed)
        k1, k2 = jax.random.split(key)
        x = jax.random.normal(k1, (N, D), dtype=jnp.float32)
        adj = jax.random.randint(k2, (N, N), 0, 2, dtype=jnp.int32)
        return {'x': x, 'adj': adj}
    _L0_gnn_all = _L0_gnn_setup()
    _L0_gnn_in = {k: v for k, v in _L0_gnn_all.items() if k in ()}
    del _L0_gnn_all

    def _L1_gnn_setup():
        import jax, jax.numpy as jnp
        import numpy as np
        N = 4096
        D_IN = 128
        D_HID = 128
        D_OUT = 128
        key = jax.random.key(seed)
        k_x, k_a, k0, k1, k2, k3 = jax.random.split(key, 6)
        x = jax.random.normal(k_x, (N, D_IN), dtype=jnp.float32)
        adj_matrix = jax.random.randint(k_a, (N, N), 0, 2, dtype=jnp.int32)
        s0 = 1.0 / np.sqrt(D_IN)
        s1 = 1.0 / np.sqrt(D_HID)
        w_self_0 = jax.random.uniform(k0, (D_HID, D_IN), jnp.float32, -s0, s0)
        w_neigh_0 = jax.random.uniform(k1, (D_HID, D_IN), jnp.float32, -s0, s0)
        w_self_1 = jax.random.uniform(k2, (D_OUT, D_HID), jnp.float32, -s1, s1)
        w_neigh_1 = jax.random.uniform(k3, (D_OUT, D_HID), jnp.float32, -s1, s1)
        return {'x': x, 'adj_matrix': adj_matrix, 'w_self_0': w_self_0, 'w_neigh_0': w_neigh_0, 'w_self_1': w_self_1, 'w_neigh_1': w_neigh_1}
    _L1_gnn_all = _L1_gnn_setup()
    _L1_gnn_in = {k: v for k, v in _L1_gnn_all.items() if k in ('w_self_0', 'w_neigh_0', 'w_self_1', 'w_neigh_1')}
    del _L1_gnn_all
    return {'x': x, 'adj': adj, 'L1_gnn_w_self_0': _L1_gnn_in['w_self_0'], 'L1_gnn_w_neigh_0': _L1_gnn_in['w_neigh_0'], 'L1_gnn_w_self_1': _L1_gnn_in['w_self_1'], 'L1_gnn_w_neigh_1': _L1_gnn_in['w_neigh_1']}

def reference(x, adj, L1_gnn_w_self_0, L1_gnn_w_neigh_0, L1_gnn_w_self_1, L1_gnn_w_neigh_1):
    import jax
    import jax.numpy as jnp

    def _L0_gnn_ref(x, adj):
        import jax, jax.numpy as jnp
        import numpy as np
        N, D = (8192, 128)
        a = adj.astype(x.dtype)
        return x + jnp.matmul(a, x)

    def _L1_gnn_ref(x, adj_matrix, w_self_0, w_neigh_0, w_self_1, w_neigh_1):
        import jax, jax.numpy as jnp
        import numpy as np
        N = 4096
        D_IN = 128
        D_HID = 128
        D_OUT = 128
        A = adj_matrix.astype(x.dtype)

        def layer(h, w_self, w_neigh):
            neigh = A @ h
            return jax.nn.relu(h @ w_self.T + neigh @ w_neigh.T)
        h = layer(x, w_self_0, w_neigh_0)
        return layer(h, w_self_1, w_neigh_1)
    x = _layernorm(x + _L0_gnn_ref(x, adj), axis=-1)
    x = _layernorm(x + _L1_gnn_ref(x, adj, L1_gnn_w_self_0, L1_gnn_w_neigh_0, L1_gnn_w_self_1, L1_gnn_w_neigh_1), axis=-1)
    return x

_drawn_inputs = setup_inputs


def setup_inputs(seed=0):
    import zlib

    import numpy as np

    out = dict(_drawn_inputs(seed))
    spreads = {}
    factors = {}
    for name, (base, spread) in spreads.items():
        noise = np.random.default_rng([zlib.crc32(name.encode()), seed]).standard_normal(out[name].shape)
        drawn = base * np.exp(spread * noise) if base else spread * noise
        out[name] = jnp.asarray(drawn.astype(out[name].dtype))
    for name, factor in factors.items():
        out[name] = (out[name] * factor).astype(out[name].dtype)
    return out
```

```python
from contextlib import ExitStack

import concourse.bass as bass
from concourse import mybir

F32 = mybir.dt.float32
F16 = mybir.dt.float16
BF16 = mybir.dt.bfloat16
F8 = mybir.dt.float8e4
I32 = mybir.dt.int32
U32 = mybir.dt.uint32
ALU = mybir.AluOpType
ACT = mybir.ActivationFunctionType
AX = mybir.AxisListType

P = 128
N = 4096
D = 128
TILES = N // P
GT = 4
GW = GT * P
GROUPS = N // GW
CHUNKS = TILES // GT
CW = GT * GW
NCHUNK = GROUPS * CHUNKS
SLOTS = 3
HELD = 4
EPS = 1e-5
SPLIT_EXP = 14
EXP_MASK = 0x7F800000
EXP_ONE = 1 << 23


def held_schedule():
    order = [(g, j) for last in range(GROUPS) for g in range(HELD) for j in range(GROUPS)
             if max(g, j) == last]
    order.sort(key=lambda b: (max(b), 0 if b[1] < max(b) else 1, b[0], b[1]))
    at, n = {}, 0
    for s in range(1, GROUPS):
        for c in range(1, CHUNKS, 2):
            if n < len(order):
                g, j = order[n]
                if g < s and (j < s - 1 or (j == s - 1 and c >= 5)):
                    at[(s, c)] = order[n]
                    n += 1
    return at, sorted(order[n:])


def graph_layers(nc, x, adj_t, wn0, wn0_t, ws0_t, w1_t, x1_dram, out):
    held_at, held_rest = held_schedule()
    held_first, held_last = {}, {}
    for b in [held_at[k] for k in sorted(held_at)] + held_rest:
        held_first.setdefault(b[0], b)
        held_last[b[0]] = b

    with ExitStack() as ctx:
        def sb(name, shape, dt):
            return ctx.enter_context(nc.sbuf_tensor(name, shape, dt))

        def sem(name):
            return ctx.enter_context(nc.semaphore(name))

        a8 = sb("a8", [P, GROUPS, TILES, GW], F8)
        stage = sb("stage", [P, SLOTS, CW], I32)
        xparts = sb("xparts", [P, TILES, 2 * D], F16)
        gparts = sb("gparts", [P, TILES, 2 * D], F16)
        rows = sb("rows", [P, TILES, D], F32)
        turned = sb("turned", [P, GW], F32)
        junk = sb("junk", [P, CW // 2], BF16)
        wn0t_sb = sb("wn0t_sb", [P, D], F32)
        ws0t_sb = sb("ws0t_sb", [P, D], F32)
        w1t_sb = sb("w1t_sb", [P, 2 * D], F32)
        ident = sb("ident", [P, P], F32)
        ones = sb("ones", [P, P], F32)
        peaks = sb("peaks", [P, 16], F32)
        bound = sb("bound", [P, 4], F32)
        brow = sb("brow", [P, 4], F32)
        clamped = sb("clamped", [P, 4], F32)
        expo = sb("expo", [P, 4], I32)
        scale = sb("scale", [P, 4], F32)
        inv = sb("inv", [P, 4], F32)
        two_sx = sb("two_sx", [P, 1], F32)
        eps_sx = sb("eps_sx", [P, 1], F32)
        eps_t = sb("eps_t", [P, 1], F32)
        stats = sb("stats", [P, GT, 6], F32)
        mv = sb("mv", [P, GT, 2], F32)
        std = sb("std", [P, GT], F32)
        rstd = sb("rstd", [P, GT], F32)
        widest = sb("widest", [P, NCHUNK], F32)

        ps = ctx.enter_context(nc.psum_tensor("ps", [P, 8, GW], F32))
        sums1 = ps[:, 0:2, :].rearrange("p b (t c) -> p (b t) c", t=2)
        MA, MB = 2, 3

        def acc_bank(g):
            return 4 + g if g < HELD else (0, 1, 4, 5)[g - HELD]

        P3_BANKS = (0, 1, 6, 7)

        g1 = xparts[:].bitcast(F32)

        x_in = [sem(f"x_in{q}") for q in range(4)]
        w_in = sem("w_in")
        adj_in = [sem(f"adj_in{k}") for k in range(SLOTS)]
        consts_ready = sem("consts_ready")
        bound_ready = sem("bound_ready")
        act_chain = sem("act_chain")
        dve_chain = sem("dve_chain")
        peaks_ready = sem("peaks_ready")
        peaks_turned = sem("peaks_turned")
        row_ready = sem("row_ready")
        spread = sem("spread")
        scale_ready = sem("scale_ready")
        x_hi = sem("x_hi")
        x_lo = sem("x_lo")
        cast_done = sem("cast_done")
        checked = sem("checked")
        pass1_done = sem("pass1_done")
        pass1_read = sem("pass1_read")
        var_ready = sem("var_ready")
        std_ready = sem("std_ready")
        x1_ready = sem("x1_ready")
        x1_turned = sem("x1_turned")
        x1t_ready = sem("x1t_ready")
        x1_stored = sem("x1_stored")
        g0_done = sem("g0_done")
        rt_done = sem("rt_done")
        rt_copied = sem("rt_copied")
        g0_hi = sem("g0_hi")
        g0_lo = sem("g0_lo")
        pass2_done = sem("pass2_done")
        h1_summed = sem("h1_summed")
        h1_ready = sem("h1_ready")
        g1u_done = sem("g1u_done")
        g1_copied = sem("g1_copied")
        u_copied = sem("u_copied")
        g1_peak = sem("g1_peak")
        g1_hi = sem("g1_hi")
        g1_lo = sem("g1_lo")
        x1_back = [sem(f"x1_back{h}") for h in range(2)]
        pass3_done = sem("pass3_done")
        pass3_read = sem("pass3_read")
        var3_ready = sem("var3_ready")
        std3_ready = sem("std3_ready")
        out_ready = sem("out_ready")
        out_stored = sem("out_stored")

        by_node = lambda t: t.rearrange("(n p) d -> p n d", p=P)
        x_nodes, x1_nodes, out_nodes = by_node(x), by_node(x1_dram), by_node(out)

        block = ctx.enter_context(nc.Block())

        @block.sync
        def _(sp):
            q = TILES // 4
            for k in range(4):
                sp.dma_start(rows[:, k * q:(k + 1) * q, :], x_nodes[:, k * q:(k + 1) * q, :]).then_inc(x_in[k], 16)
            sp.dma_start(turned[:, 0:D], wn0).then_inc(w_in, 16)
            sp.dma_start(wn0t_sb[:], wn0_t).then_inc(w_in, 16)
            sp.dma_start(ws0t_sb[:], ws0_t).then_inc(w_in, 16)
            sp.dma_start(w1t_sb[:], w1_t).then_inc(w_in, 16)
            for n in range(SLOTS):
                sp.dma_start(stage[:, n, :], adj_t[n]).then_inc(adj_in[n], 16)
            rounds = (NCHUNK - SLOTS) // SLOTS
            with sp.Fori(0, rounds) as r:
                for k in range(SLOTS):
                    sp.wait_ge(cast_done, r * SLOTS + (k + 1))
                    sp.wait_ge(checked, r * SLOTS + (k + 1))
                    sp.dma_start(stage[:, k, :], adj_t[bass.ds(r * SLOTS + (SLOTS + k), 1)].rearrange("o p c -> p (o c)")
                                 ).then_inc(adj_in[k], 16)
            for n in range(SLOTS + rounds * SLOTS, NCHUNK):
                sp.wait_ge(cast_done, n - SLOTS + 1)
                sp.wait_ge(checked, n - SLOTS + 1)
                sp.dma_start(stage[:, n % SLOTS, :], adj_t[n]).then_inc(adj_in[n % SLOTS], 16)
            half = TILES // 2
            for h in range(2):
                sp.wait_ge(g1_hi, GROUPS // 2 * (h + 1))
                sp.wait_ge(g1_lo, GROUPS // 2 * (h + 1))
                sp.wait_ge(x1_stored, 16 * GROUPS)
                sp.dma_start(g1[:, h * half:(h + 1) * half, :], x1_nodes[:, h * half:(h + 1) * half, :]
                             ).then_inc(x1_back[h], 16)
            stores = 0
            for t in range(TILES):
                if t % GT == GT - 1 and t < TILES - GT:
                    sp.wait_ge(out_ready, t + 1)
                    sp.dma_start(out_nodes[:, t + 1 - GT:t + 1, :], rows[:, t + 1 - GT:t + 1, :]).then_inc(out_stored, 16)
                    stores += 1
                elif t >= TILES - GT:
                    sp.wait_ge(out_ready, t + 1)
                    sp.dma_start(out_nodes[:, t:t + 1, :], rows[:, t:t + 1, :]).then_inc(out_stored, 16)
                    stores += 1
            sp.wait_ge(out_stored, 16 * stores)

        @block.gpsimd
        def _(pool):
            nc.gpsimd.memset(ident[:], 0.0).then_inc(consts_ready, 1)
            nc.gpsimd.memset(ones[:], 1.0).then_inc(consts_ready, 1)
            nc.gpsimd.memset(eps_t[:], EPS).then_inc(consts_ready, 1)
            pool.wait_ge(consts_ready, 3)
            nc.gpsimd.affine_select(out=ident[:], in_=ident[:], compare_op=ALU.not_equal, fill=1.0, base=0,
                                    pattern=[[-1, P]], channel_multiplier=1).then_inc(consts_ready, 1)

        @block.scalar
        def _(act):
            act.wait_ge(w_in, 16 * 4)
            nc.scalar.activation(turned[:, D:2 * D], turned[:, 0:D], ACT.Square, accum_out=peaks[:, 15:16]).then_inc(act_chain, 1)
            act.wait_ge(act_chain, 1)
            nc.scalar.activation(bound[:, 1:2], peaks[:, 15:16], ACT.Sqrt, scale=float(D)).then_inc(bound_ready, 1)

            def cast(n):
                act.wait_ge(adj_in[n % SLOTS], 16 * (n // SLOTS + 1))
                g, c = divmod(n, CHUNKS)
                nc.scalar.activation(a8[:, g, c * GT:(c + 1) * GT, :],
                                     stage[:, n % SLOTS, :].rearrange("p (t i) -> p t i", t=GT),
                                     ACT.Copy, saturate=False).then_inc(cast_done, 1)

            def group_std(s):
                act.wait_ge(var_ready, s + 1)
                nc.scalar.activation(std[:], mv[:, :, 1], ACT.Sqrt, bias=eps_sx[:]).then_inc(std_ready, 1)

            def copy_x1t(s):
                act.wait_ge(x1_turned, s + 1)
                nc.scalar.activation(turned[:], ps[:, MA, :], ACT.Copy).then_inc(x1t_ready, 1)
                act.wait_ge(x1_ready, s + 1)
                act.dma_start(x1_nodes[:, s * GT:(s + 1) * GT, :], rows[:, s * GT:(s + 1) * GT, :]).then_inc(x1_stored, 16)

            def split_g0(s):
                act.wait_ge(g0_done, s + 1)
                nc.scalar.activation(gparts[:, s * GT:(s + 1) * GT, 0:D], ps[:, MB, :].rearrange("p (t d) -> p t d", t=GT),
                                     ACT.Copy, scale=scale[:, 1:2]).then_inc(g0_hi, 1)

            def copy_rt(s):
                act.wait_ge(rt_done, s + 1)
                act.wait_ge(x1_stored, 16 * (s + 1))
                nc.scalar.activation(rows[:, s * GT:(s + 1) * GT, :].rearrange("p t d -> p (t d)"), ps[:, MA, :],
                                     ACT.Copy).then_inc(rt_copied, 1)

            def split_x(c):
                nc.scalar.activation(xparts[:, c * GT:(c + 1) * GT, 0:D], rows[:, c * GT:(c + 1) * GT, :],
                                     ACT.Copy, scale=scale[:, 0:1]).then_inc(x_hi, 1)

            for s in range(GROUPS):
                for c in range(CHUNKS):
                    cast(s * CHUNKS + c)
                    if s == 0:
                        if c == 0:
                            act.wait_ge(scale_ready, 1)
                        split_x(c)
                    elif c == 0:
                        group_std(s - 1)
                    elif c == 1:
                        copy_x1t(s - 1)
                    elif c == 3:
                        split_g0(s - 1)
                        copy_rt(s - 1)
            group_std(GROUPS - 1)
            copy_x1t(GROUPS - 1)
            split_g0(GROUPS - 1)
            copy_rt(GROUPS - 1)

            for g in range(GROUPS):
                act.wait_ge(h1_summed, g + 1)
                if g == 0:
                    act.wait_ge(rt_done, GROUPS)
                else:
                    act.wait_ge(g1u_done, g)
                nc.scalar.activation(turned[:], rows[:, g * GT:(g + 1) * GT, :].rearrange("p t d -> p (t d)"),
                                     ACT.Relu).then_inc(h1_ready, 1)
                act.wait_ge(g1u_done, g + 1)
                nc.scalar.activation(g1[:, g * GT:(g + 1) * GT, :], ps[:, MA, :].rearrange("p (t d) -> p t d", t=GT),
                                     ACT.Copy).then_inc(g1_copied, 1)
                act.wait_ge(h1_ready, g + 1)
                nc.scalar.activation(rows[:, g * GT:(g + 1) * GT, :], ps[:, MB, :].rearrange("p (t d) -> p t d", t=GT),
                                     ACT.Copy).then_inc(u_copied, 1)

            act.wait_ge(scale_ready, 2)
            act.wait_ge(pass2_done, GROUPS)
            act.wait_ge(g1_copied, GROUPS)
            for g in range(GROUPS):
                nc.scalar.activation(gparts[:, g * GT:(g + 1) * GT, 0:D], g1[:, g * GT:(g + 1) * GT, :],
                                     ACT.Copy, scale=scale[:, 2:3]).then_inc(g1_hi, 1)
            for t in range(TILES):
                act.wait_ge(var3_ready, t + 1)
                nc.scalar.activation(std[:, 0:1], mv[:, 0, 1:2], ACT.Sqrt, bias=eps_t[:]).then_inc(std3_ready, 1)

        @block.tensor
        def _(pe):
            def turn_peaks(cols, banks_free):
                for sem_, value in banks_free:
                    pe.wait_ge(sem_, value)
                for k, col in enumerate(cols):
                    mm = pe.matmul(ps[0:1, MA, k * P:(k + 1) * P], bound[:, col:col + 1], ident[:], start=True, stop=True)
                mm.then_inc(peaks_turned, 1)

            def spread_peaks(count, n):
                pe.wait_ge(row_ready, n)
                pe.matmul(ps[:, MB, 0:count], ones[0:1, :], brow[0:1, 0:count], start=True, stop=True).then_inc(spread, 1)

            def pass1_chunk(s, c):
                pe.wait_ge(cast_done, s * CHUNKS + c + 1)
                if s == 0:
                    pe.wait_ge(x_lo, c + 1)
                elif c == 0:
                    pe.wait_ge(pass1_read, s)
                for j in range(c * GT, (c + 1) * GT):
                    for t in range(GT):
                        mm = pe.matmul(sums1[:, t, :], a8[:, s, j, t * P:(t + 1) * P], xparts[:, j, :],
                                       start=(j == 0 and t % 2 == 0), stop=(j == TILES - 1), skip_group_check=True)
                if c == CHUNKS - 1:
                    mm.then_inc(pass1_done, 1)

            def turn_x1(s):
                pe.wait_ge(x1_ready, s + 1)
                if s >= 1:
                    pe.wait_ge(rt_copied, s)
                for t in range(GT):
                    mm = pe.transpose(ps[:, MA, t * P:(t + 1) * P], rows[:, s * GT + t, :], ident[:])
                mm.then_inc(x1_turned, 1)

            def small_products0(s):
                pe.wait_ge(x1t_ready, s + 1)
                if s >= 1:
                    pe.wait_ge(g0_lo, s)
                for t in range(GT):
                    mm = pe.matmul(ps[:, MB, t * P:(t + 1) * P], turned[:, t * P:(t + 1) * P], wn0t_sb[:],
                                   start=True, stop=True)
                mm.then_inc(g0_done, 1)
                pe.matmul(ps[:, MA, :], ws0t_sb[:], turned[:], start=True, stop=True).then_inc(rt_done, 1)

            def pass2_block(g, jg):
                pe.wait_ge(g0_lo, jg + 1)
                first = held_first[g] == (g, jg) if g < HELD else jg == 0
                last = held_last[g] == (g, jg) if g < HELD else jg == GROUPS - 1
                for j in range(jg * GT, (jg + 1) * GT):
                    for part in range(2):
                        mm = pe.matmul(ps[:, acc_bank(g), :], gparts[:, j, part * D:(part + 1) * D], a8[:, g, j, :],
                                       start=(first and j == jg * GT and part == 0),
                                       stop=(last and j == jg * GT + GT - 1 and part == 1))
                if last:
                    mm.then_inc(pass2_done, 1)

            def small_products1(g):
                pe.wait_ge(h1_ready, g + 1)
                if g == 0:
                    pe.wait_ge(rt_copied, GROUPS)
                else:
                    pe.wait_ge(u_copied, g)
                for part, bank in enumerate((MA, MB)):
                    for t in range(GT):
                        mm = pe.matmul(ps[:, bank, t * P:(t + 1) * P], turned[:, t * P:(t + 1) * P],
                                       w1t_sb[:, part * D:(part + 1) * D], start=True, stop=True)
                mm.then_inc(g1u_done, 1)

            pe.wait_ge(consts_ready, 4)
            pe.wait_ge(w_in, 16 * 4)
            turn_peaks((0, 1), [(peaks_ready, 1), (bound_ready, 1)])
            spread_peaks(2, 1)
            for s in range(GROUPS):
                for c in range(CHUNKS):
                    pass1_chunk(s, c)
                    if s and c == 0:
                        turn_x1(s - 1)
                    if s and c == 2:
                        small_products0(s - 1)
                    if (s, c) in held_at:
                        pass2_block(*held_at[(s, c)])
            first_rest = [b for b in held_rest if b[1] < GROUPS - 1]
            last_rest = [b for b in held_rest if b[1] == GROUPS - 1]
            half = len(first_rest) // 2
            for b in first_rest[:half]:
                pass2_block(*b)
            turn_x1(GROUPS - 1)
            for b in first_rest[half:]:
                pass2_block(*b)
            small_products0(GROUPS - 1)
            for g, jg in last_rest:
                pass2_block(g, jg)
                if g >= 1:
                    small_products1(g - 1)
            for g in range(HELD, GROUPS):
                if g >= HELD + 2:
                    pe.wait_ge(h1_summed, g - HELD - 2 + 1)
                else:
                    pe.wait_ge(pass1_read, GROUPS)
                for jg in range(GROUPS):
                    pass2_block(g, jg)
                small_products1(g - 1)
            small_products1(GROUPS - 1)
            turn_peaks((2,), [(peaks_ready, 2), (g1_copied, GROUPS)])
            pe.wait_ge(u_copied, GROUPS)
            spread_peaks(1, 2)
            for t in range(TILES):
                bank = P3_BANKS[t % 4]
                if t >= 4:
                    pe.wait_ge(pass3_read, t - 3)
                else:
                    pe.wait_ge(h1_summed, GROUPS)
                for j in range(TILES):
                    if t == 0 and j % GT == 0:
                        pe.wait_ge(g1_lo, j // GT + 1)
                    mm = pe.matmul(ps[:, bank, 0:2 * D], a8[:, t // GT, j, (t % GT) * P:(t % GT + 1) * P], gparts[:, j, :],
                                   start=(j == 0), stop=(j == TILES - 1))
                mm.then_inc(pass3_done, 1)

        @block.vector
        def _(dve):
            steps = [0]

            def link(ins):
                steps[0] += 1
                ins.then_inc(dve_chain, 1)
                dve.wait_ge(dve_chain, steps[0])

            def make_scales(first, count, n):
                dve.wait_ge(peaks_turned, n)
                nc.vector.tensor_reduce(brow[0:1, 0:count], ps[0:1, MA, 0:count * P].rearrange("p (k i) -> p k i", k=count),
                                        AX.X, ALU.max).then_inc(row_ready, 1)
                dve.wait_ge(spread, n)
                cols = slice(first, first + count)
                link(nc.vector.tensor_scalar(clamped[:, cols], ps[:, MB, 0:count], 2.0 ** -36, 2.0 ** 100, ALU.max, ALU.min))
                link(nc.vector.tensor_scalar(expo[:, cols], clamped[:, cols].bitcast(I32), EXP_MASK, None, ALU.bitwise_and))
                link(nc.vector.tensor_scalar(inv[:, cols].bitcast(I32), expo[:, cols], float(SPLIT_EXP * EXP_ONE), None,
                                             ALU.subtract))
                link(nc.vector.tensor_scalar(scale[:, cols].bitcast(I32), expo[:, cols], -1.0,
                                             float((2 * 127 + SPLIT_EXP) * EXP_ONE), ALU.mult, ALU.add))

            def check_range(n):
                dve.wait_ge(adj_in[n % SLOTS], 16 * (n // SLOTS + 1))
                if n:
                    dve.wait_ge(checked, n)
                v = stage[:, n % SLOTS, :].bitcast(U32)
                nc.vector.tensor_tensor_reduce(junk[:], v[:, 0:CW // 2], v[:, CW // 2:CW], 1.0, 0.0, ALU.add, ALU.max,
                                               widest[:, n:n + 1]).then_inc(checked, 1)

            def norm_stats(s):
                r = rows[:, s * GT:(s + 1) * GT, :]
                dve.wait_ge(pass1_done, s + 1)
                link(nc.vector.scalar_tensor_tensor(r, r, two_sx[:], sums1[:, :, 0:D], ALU.mult, ALU.add))
                nc.vector.tensor_tensor(r, r, sums1[:, :, D:2 * D], ALU.add).then_inc(pass1_read, 1)
                dve.wait_ge(pass1_read, s + 1)
                for t in range(GT):
                    ins = nc.vector.bn_stats(stats[:, t, :], rows[:, s * GT + t, :])
                link(ins)
                for t in range(GT):
                    ins = nc.vector.bn_aggr(mv[:, t, :], stats[:, t, :])
                ins.then_inc(var_ready, 1)

            def normalize(s):
                dve.wait_ge(std_ready, s + 1)
                link(nc.vector.reciprocal(rstd[:], std[:]))
                for t in range(GT):
                    r = rows[:, s * GT + t, :]
                    ins = nc.vector.tensor_scalar(r, r, mv[:, t, 0:1], rstd[:, t:t + 1], ALU.subtract, ALU.mult)
                ins.then_inc(x1_ready, 1)

            def split_g0_lo(s):
                dve.wait_ge(g0_hi, s + 1)
                tiles = slice(s * GT, (s + 1) * GT)
                nc.vector.scalar_tensor_tensor(gparts[:, tiles, D:2 * D], ps[:, MB, :].rearrange("p (t d) -> p t d", t=GT),
                                               scale[:, 1:2], gparts[:, tiles, 0:D], ALU.mult, ALU.subtract
                                               ).then_inc(g0_lo, 1)

            for q in range(4):
                dve.wait_ge(x_in[q], 16)
                ins = nc.vector.tensor_reduce(peaks[:, q:q + 1], rows[:, 8 * q:8 * (q + 1), :], AX.XY, ALU.max,
                                              apply_absolute_value=True)
            link(ins)
            nc.vector.tensor_reduce(bound[:, 0:1], peaks[:, 0:4], AX.X, ALU.max).then_inc(peaks_ready, 1)
            make_scales(0, 2, 1)
            nc.vector.tensor_scalar(two_sx[:], scale[:, 0:1], 2.0, None, ALU.mult)
            nc.vector.tensor_scalar(eps_sx[:], scale[:, 0:1], scale[:, 0:1], EPS, ALU.mult, ALU.mult
                                    ).then_inc(scale_ready, 1)
            for s in range(GROUPS):
                for c in range(CHUNKS):
                    if s == 0:
                        dve.wait_ge(x_hi, c + 1)
                        tiles = slice(c * GT, (c + 1) * GT)
                        nc.vector.scalar_tensor_tensor(xparts[:, tiles, D:2 * D], rows[:, tiles, :], scale[:, 0:1],
                                                       xparts[:, tiles, 0:D], ALU.mult, ALU.subtract).then_inc(x_lo, 1)
                    elif c == 0:
                        norm_stats(s - 1)
                    elif c == 1:
                        normalize(s - 1)
                    elif c == 4:
                        split_g0_lo(s - 1)
                    check_range(s * CHUNKS + c)
            norm_stats(GROUPS - 1)
            normalize(GROUPS - 1)
            split_g0_lo(GROUPS - 1)

            for g in range(GROUPS):
                dve.wait_ge(pass2_done, g + 1)
                dve.wait_ge(rt_copied, g + 1)
                r = rows[:, g * GT:(g + 1) * GT, :].rearrange("p t d -> p (t d)")
                nc.vector.scalar_tensor_tensor(r, ps[:, acc_bank(g), :], inv[:, 1:2], r, ALU.mult, ALU.add
                                               ).then_inc(h1_summed, 1)
                dve.wait_ge(g1_copied, g + 1)
                nc.vector.tensor_reduce(peaks[:, g:g + 1], g1[:, g * GT:(g + 1) * GT, :], AX.XY, ALU.max,
                                        apply_absolute_value=True).then_inc(g1_peak, 1)
            dve.wait_ge(g1_peak, GROUPS)
            nc.vector.tensor_reduce(bound[:, 2:3], peaks[:, 0:GROUPS], AX.X, ALU.max).then_inc(peaks_ready, 1)
            make_scales(2, 1, 2)
            nc.vector.memset(peaks[:, 15:16], 0.0).then_inc(scale_ready, 1)
            for g in range(GROUPS):
                dve.wait_ge(g1_hi, g + 1)
                tiles = slice(g * GT, (g + 1) * GT)
                nc.vector.scalar_tensor_tensor(gparts[:, tiles, D:2 * D], g1[:, tiles, :], scale[:, 2:3],
                                               gparts[:, tiles, 0:D], ALU.mult, ALU.subtract).then_inc(g1_lo, 1)
            for t in range(TILES):
                r = rows[:, t, :]
                bank = P3_BANKS[t % 4]
                dve.wait_ge(pass3_done, t + 1)
                dve.wait_ge(u_copied, t // GT + 1)
                link(nc.vector.scalar_tensor_tensor(r, ps[:, bank, 0:D], inv[:, 2:3], r, ALU.mult, ALU.add))
                nc.vector.scalar_tensor_tensor(r, ps[:, bank, D:2 * D], inv[:, 2:3], r, ALU.mult, ALU.add
                                               ).then_inc(pass3_read, 1)
                dve.wait_ge(pass3_read, t + 1)
                dve.wait_ge(x1_back[t // (TILES // 2)], 16)
                link(nc.vector.scalar_tensor_tensor(r, r, 0.0, g1[:, t, :], ALU.max, ALU.add))
                link(nc.vector.bn_stats(stats[:, 0, :], r))
                nc.vector.bn_aggr(mv[:, 0, :], stats[:, 0, :]).then_inc(var3_ready, 1)
                dve.wait_ge(std3_ready, t + 1)
                link(nc.vector.reciprocal(rstd[:, 0:1], std[:, 0:1]))
                nc.vector.tensor_scalar(r, r, mv[:, 0, 0:1], rstd[:, 0:1], ALU.subtract, ALU.mult).then_inc(out_ready, 1)


def kernel(x, adj, L1_gnn_w_self_0, L1_gnn_w_neigh_0, L1_gnn_w_self_1, L1_gnn_w_neigh_1):
    import numpy as np
    import concourse.bacc as bacc
    from concourse.bass_utils import run_bass_kernel_spmd

    adj_t = np.ascontiguousarray(
        np.asarray(adj).reshape(GROUPS, GW, CHUNKS, GT, P).transpose(0, 2, 4, 3, 1)).reshape(NCHUNK, P, CW)
    wn1_t, ws1_t = np.asarray(L1_gnn_w_neigh_1).T, np.asarray(L1_gnn_w_self_1).T
    arrays = {
        "in_x": np.ascontiguousarray(x),
        "in_adj_t": adj_t,
        "in_wn0": np.ascontiguousarray(L1_gnn_w_neigh_0),
        "in_wn0_t": np.ascontiguousarray(np.asarray(L1_gnn_w_neigh_0).T),
        "in_ws0_t": np.ascontiguousarray(np.asarray(L1_gnn_w_self_0).T),
        "in_w1_t": np.ascontiguousarray(np.concatenate([wn1_t, ws1_t], axis=1)),
    }
    nc = bacc.Bacc("TRN2", target_bir_lowering=False, num_devices=1)
    aps = [nc.dram_tensor(k, a.shape, mybir.dt.from_np(a.dtype), kind="ExternalInput").ap() for k, a in arrays.items()]
    x1_dram = nc.dram_tensor("x1_dram", (N, D), F32, kind="Internal").ap()
    out = nc.dram_tensor("out_0", (N, D), F32, kind="ExternalOutput").ap()
    graph_layers(nc, *aps, x1_dram, out)
    r = run_bass_kernel_spmd(nc, [arrays], core_ids=[0])
    return r.results[0]["out_0"]
```

```python
from contextlib import ExitStack

import concourse.bass as bass
from concourse import mybir

F32 = mybir.dt.float32
F16 = mybir.dt.float16
BF16 = mybir.dt.bfloat16
F8 = mybir.dt.float8e4
I32 = mybir.dt.int32
U32 = mybir.dt.uint32
ALU = mybir.AluOpType
ACT = mybir.ActivationFunctionType
AX = mybir.AxisListType

P = 128
N = 4096
D = 128
TILES = N // P
GT = 4
GW = GT * P
GROUPS = N // GW
CHUNKS = TILES // GT
CW = GT * GW
NCHUNK = GROUPS * CHUNKS
SLOTS = 3
HELD = 5
ACT_TILES = 3
EPS = 1e-5
C_STATS, C_STD, C_NORM, C_TURN, C_COPY, C_SMALL, C_SPLIT, C_SELF, C_COPY_RT = 0, 1, 1, 2, 3, 4, 5, 6, 7
HELD_CHUNKS = {0: 2, 3: 1, 6: 1, 7: 1}
LAST = GROUPS - 1
SPLIT_EXP = 14
EXP_MASK = 0x7F800000
EXP_ONE = 1 << 23


def held_schedule():
    order = sorted(((g, j) for g in range(HELD) for j in range(GROUPS)),
                   key=lambda b: (max(b), b[1] == max(b), b))
    at, n = {}, 0
    for s in range(1, GROUPS):
        for c in HELD_CHUNKS:
            g, j = order[n]
            for _ in range(HELD_CHUNKS[c]):
                g, j = order[n]
                if g < s and (j < s - 1 or (j == s - 1 and c > C_SPLIT)):
                    at.setdefault((s, c), []).append(order[n])
                    n += 1
    return at, sorted(order[n:])


def graph_layers(nc, x, adj_t, wn0, wn0_t, ws0_t, w1_t, x1_dram, out):
    held_at, held_rest = held_schedule()
    held_first, held_last = {}, {}
    for b in [b for k in sorted(held_at) for b in held_at[k]] + held_rest:
        held_first.setdefault(b[0], b)
        held_last[b[0]] = b

    with ExitStack() as ctx:
        def sb(name, shape, dt):
            return ctx.enter_context(nc.sbuf_tensor(name, shape, dt))

        def sem(name):
            return ctx.enter_context(nc.semaphore(name))

        a8 = sb("a8", [P, GROUPS, TILES, GW], F8)
        stage = sb("stage", [P, SLOTS, CW], I32)
        xparts = sb("xparts", [P, TILES, 2 * D], F16)
        gparts = sb("gparts", [P, TILES, 2 * D], F16)
        rows = sb("rows", [P, TILES, D], F32)
        turned = sb("turned", [P, GW], F32)
        junk = sb("junk", [P, CW // 2], BF16)
        wn0t_sb = sb("wn0t_sb", [P, D], F32)
        ws0t_sb = sb("ws0t_sb", [P, D], F32)
        w1t_sb = sb("w1t_sb", [P, 2 * D], F32)
        ident = sb("ident", [P, P], F32)
        ones = sb("ones", [P, P], F32)
        peaks = sb("peaks", [P, 16], F32)
        bound = sb("bound", [P, 4], F32)
        brow = sb("brow", [P, 4], F32)
        clamped = sb("clamped", [P, 4], F32)
        expo = sb("expo", [P, 4], I32)
        scale = sb("scale", [P, 4], F32)
        inv = sb("inv", [P, 4], F32)
        cols = sb("cols", [P, 4], F32)
        two_sx = cols[:, 0:1]
        eps_sx = cols[:, 1:2]
        eps4_sx = cols[:, 2:3]
        eps4 = cols[:, 3:4]
        stats = sb("stats", [P, GT, 6], F32)
        mv = sb("mv", [P, GT, 2], F32)
        std2 = sb("std2", [P, GT], F32)
        quot = sb("quot", [P, GT], F32)
        std = sb("std", [P, GT], F32)
        rstd = sb("rstd", [P, GT], F32)
        widest = sb("widest", [P, NCHUNK], F32)

        ps = ctx.enter_context(nc.psum_tensor("ps", [P, 8, GW], F32))
        sums1 = ps[:, 0:2, :].rearrange("p b (t c) -> p (b t) c", t=2)
        MA, MB = 2, 1

        def acc_bank(g):
            return 3 + g if g < HELD else (0, 3, 4)[g - HELD]

        P3_BANKS = (5, 6, 7, 0)

        g1 = xparts[:].bitcast(F32)
        g1parts = stage[:].rearrange("p s c -> p (s c)").bitcast(F16)[:, 0:TILES * 2 * D].rearrange(
            "p (t d) -> p t d", t=TILES)

        x_in = [sem(f"x_in{q}") for q in range(4)]
        w_in = sem("w_in")
        adj_in = [sem(f"adj_in{k}") for k in range(SLOTS)]
        consts_ready = sem("consts_ready")
        bound_ready = sem("bound_ready")
        act_chain = sem("act_chain")
        dve_chain = sem("dve_chain")
        peaks_ready = sem("peaks_ready")
        peaks_turned = sem("peaks_turned")
        row_ready = sem("row_ready")
        spread = sem("spread")
        scale_ready = sem("scale_ready")
        x_hi = sem("x_hi")
        x_lo = sem("x_lo")
        cast_act = sem("cast_act")
        cast_dve = sem("cast_dve")
        checked = sem("checked")
        pass1_done = sem("pass1_done")
        pass1_read = sem("pass1_read")
        var_ready = sem("var_ready")
        std_ready = sem("std_ready")
        x1_ready = sem("x1_ready")
        x1_turned = sem("x1_turned")
        x1t_ready = sem("x1t_ready")
        x1_stored = sem("x1_stored")
        g0_done = sem("g0_done")
        rt_done = sem("rt_done")
        rt_copied = sem("rt_copied")
        g0_hi = sem("g0_hi")
        g0_lo = sem("g0_lo")
        pass2_done = sem("pass2_done")
        h1_summed = sem("h1_summed")
        h1_ready = sem("h1_ready")
        g1u_done = sem("g1u_done")
        g1_copied = sem("g1_copied")
        u_copied = sem("u_copied")
        g1_peak = sem("g1_peak")
        g1_hi = sem("g1_hi")
        g1_lo = sem("g1_lo")
        x1_back = [sem(f"x1_back{h}") for h in range(2)]
        pass3_done = sem("pass3_done")
        pass3_read = sem("pass3_read")
        var3_ready = sem("var3_ready")
        std3_ready = sem("std3_ready")
        out_ready = sem("out_ready")
        out_stored = sem("out_stored")

        by_node = lambda t: t.rearrange("(n p) d -> p n d", p=P)
        x_nodes, x1_nodes, out_nodes = by_node(x), by_node(x1_dram), by_node(out)

        block = ctx.enter_context(nc.Block())

        @block.sync
        def _(sp):
            q = TILES // 4
            for k in range(4):
                sp.dma_start(rows[:, k * q:(k + 1) * q, :], x_nodes[:, k * q:(k + 1) * q, :]).then_inc(x_in[k], 16)
            sp.dma_start(turned[:, 0:D], wn0).then_inc(w_in, 16)
            sp.dma_start(wn0t_sb[:], wn0_t).then_inc(w_in, 16)
            sp.dma_start(ws0t_sb[:], ws0_t).then_inc(w_in, 16)
            sp.dma_start(w1t_sb[:], w1_t).then_inc(w_in, 16)
            for n in range(SLOTS):
                sp.dma_start(stage[:, n, :], adj_t[n]).then_inc(adj_in[n], 16)
            rounds = (NCHUNK - SLOTS) // SLOTS
            with sp.Fori(0, rounds) as r:
                for k in range(SLOTS):
                    sp.wait_ge(cast_act, r * SLOTS + (k + 1))
                    sp.wait_ge(cast_dve, r * SLOTS + (k + 1))
                    sp.wait_ge(checked, r * SLOTS + (k + 1))
                    sp.dma_start(stage[:, k, :], adj_t[bass.ds(r * SLOTS + (SLOTS + k), 1)].rearrange("o p c -> p (o c)")
                                 ).then_inc(adj_in[k], 16)
            for n in range(SLOTS + rounds * SLOTS, NCHUNK):
                sp.wait_ge(cast_act, n - SLOTS + 1)
                sp.wait_ge(cast_dve, n - SLOTS + 1)
                sp.wait_ge(checked, n - SLOTS + 1)
                sp.dma_start(stage[:, n % SLOTS, :], adj_t[n]).then_inc(adj_in[n % SLOTS], 16)
            half = TILES // 2
            for h in range(2):
                sp.wait_ge(g1_hi, GROUPS // 2 * (h + 1))
                sp.wait_ge(g1_lo, GROUPS // 2 * (h + 1))
                sp.wait_ge(x1_stored, 16 * GROUPS)
                sp.dma_start(g1[:, h * half:(h + 1) * half, :], x1_nodes[:, h * half:(h + 1) * half, :]
                             ).then_inc(x1_back[h], 16)
            stores = 0
            for t in range(TILES):
                if t % GT == GT - 1 and t < TILES - GT:
                    sp.wait_ge(out_ready, t + 1)
                    sp.dma_start(out_nodes[:, t + 1 - GT:t + 1, :], rows[:, t + 1 - GT:t + 1, :]).then_inc(out_stored, 16)
                    stores += 1
                elif t >= TILES - GT:
                    sp.wait_ge(out_ready, t + 1)
                    sp.dma_start(out_nodes[:, t:t + 1, :], rows[:, t:t + 1, :]).then_inc(out_stored, 16)
                    stores += 1
            sp.wait_ge(out_stored, 16 * stores)

        @block.gpsimd
        def _(pool):
            nc.gpsimd.memset(ident[:], 0.0).then_inc(consts_ready, 1)
            nc.gpsimd.memset(ones[:], 1.0).then_inc(consts_ready, 1)
            nc.gpsimd.memset(eps4, 4 * EPS).then_inc(consts_ready, 1)
            pool.wait_ge(consts_ready, 3)
            nc.gpsimd.affine_select(out=ident[:], in_=ident[:], compare_op=ALU.not_equal, fill=1.0, base=0,
                                    pattern=[[-1, P]], channel_multiplier=1).then_inc(consts_ready, 1)

        @block.scalar
        def _(act):
            act.wait_ge(w_in, 16 * 4)
            nc.scalar.activation(turned[:, D:2 * D], turned[:, 0:D], ACT.Square, accum_out=peaks[:, 15:16]).then_inc(act_chain, 1)
            act.wait_ge(act_chain, 1)
            nc.scalar.activation(bound[:, 1:2], peaks[:, 15:16], ACT.Sqrt, scale=float(D)).then_inc(bound_ready, 1)

            def cast(n):
                act.wait_ge(adj_in[n % SLOTS], 16 * (n // SLOTS + 1))
                g, c = divmod(n, CHUNKS)
                nc.scalar.activation(a8[:, g, c * GT:c * GT + ACT_TILES, :],
                                     stage[:, n % SLOTS, 0:ACT_TILES * GW].rearrange("p (t i) -> p t i", t=ACT_TILES),
                                     ACT.Copy, saturate=False).then_inc(cast_act, 1)

            def group_std(s):
                act.wait_ge(var_ready, s + 1)
                nc.scalar.activation(std2[:], mv[:, :, 1], ACT.Sqrt, bias=eps4_sx, scale=4.0).then_inc(std_ready, 1)

            def copy_x1t(s):
                act.wait_ge(x1_turned, s + 1)
                nc.scalar.activation(turned[:], ps[:, MA, :], ACT.Copy).then_inc(x1t_ready, 1)
                act.wait_ge(x1_ready, s + 1)
                act.dma_start(x1_nodes[:, s * GT:(s + 1) * GT, :], rows[:, s * GT:(s + 1) * GT, :]).then_inc(x1_stored, 16)

            def split_g0(s):
                act.wait_ge(g0_done, s + 1)
                nc.scalar.activation(gparts[:, s * GT:(s + 1) * GT, 0:D], ps[:, MA, :].rearrange("p (t d) -> p t d", t=GT),
                                     ACT.Copy, scale=scale[:, 1:2]).then_inc(g0_hi, 1)

            def copy_rt(s):
                act.wait_ge(rt_done, s + 1)
                act.wait_ge(x1_stored, 16 * (s + 1))
                nc.scalar.activation(rows[:, s * GT:(s + 1) * GT, :].rearrange("p t d -> p (t d)"), ps[:, MA, :],
                                     ACT.Copy).then_inc(rt_copied, 1)

            def split_x(c):
                nc.scalar.activation(xparts[:, c * GT:(c + 1) * GT, 0:D], rows[:, c * GT:(c + 1) * GT, :],
                                     ACT.Copy, scale=scale[:, 0:1]).then_inc(x_hi, 1)

            for n in range(SLOTS):
                cast(n)
            act.wait_ge(scale_ready, 1)
            for s in range(GROUPS):
                for c in range(CHUNKS):
                    if s == 0:
                        split_x(c)
                    n = s * CHUNKS + c
                    if n >= SLOTS:
                        cast(n)
                    if s:
                        if c == C_STD:
                            group_std(s - 1)
                        if c == C_COPY:
                            copy_x1t(s - 1)
                        if c == C_SPLIT:
                            split_g0(s - 1)
                        if c == C_COPY_RT:
                            copy_rt(s - 1)
            group_std(GROUPS - 1)
            copy_x1t(GROUPS - 1)
            split_g0(GROUPS - 1)
            copy_rt(GROUPS - 1)

            def hidden(g):
                act.wait_ge(h1_summed, g + 1)
                if g == 0:
                    act.wait_ge(rt_done, GROUPS)
                else:
                    act.wait_ge(g1u_done, g)
                nc.scalar.activation(turned[:], rows[:, g * GT:(g + 1) * GT, :].rearrange("p t d -> p (t d)"),
                                     ACT.Relu).then_inc(h1_ready, 1)
                act.wait_ge(g1u_done, g + 1)
                nc.scalar.activation(g1[:, g * GT:(g + 1) * GT, :], ps[:, MA, :].rearrange("p (t d) -> p t d", t=GT),
                                     ACT.Copy).then_inc(g1_copied, 1)
                act.wait_ge(h1_ready, g + 1)
                nc.scalar.activation(rows[:, g * GT:(g + 1) * GT, :], ps[:, MB, :].rearrange("p (t d) -> p t d", t=GT),
                                     ACT.Copy).then_inc(u_copied, 1)

            def split_g1(g, col):
                act.wait_ge(g1_copied, g + 1)
                nc.scalar.activation(g1parts[:, g * GT:(g + 1) * GT, 0:D], g1[:, g * GT:(g + 1) * GT, :],
                                     ACT.Copy, scale=scale[:, col:col + 1]).then_inc(g1_hi, 1)

            for g in range(LAST):
                hidden(g)
            act.wait_ge(scale_ready, 2)
            act.wait_ge(checked, NCHUNK)
            act.wait_ge(cast_dve, NCHUNK)
            for g in range(LAST):
                split_g1(g, 2)
            hidden(LAST)
            act.wait_ge(scale_ready, 3)
            split_g1(LAST, 3)
            for t in range(TILES):
                act.wait_ge(var3_ready, t + 1)
                nc.scalar.activation(std2[:, t % 2:t % 2 + 1], mv[:, t % 2, 1:2], ACT.Sqrt, bias=eps4, scale=4.0).then_inc(std3_ready, 1)

        @block.tensor
        def _(pe):
            def turn_peaks(cols, n):
                pe.wait_ge(peaks_ready, n)
                for k, col in enumerate(cols):
                    mm = pe.matmul(ps[0:1, MA, k * P:(k + 1) * P], bound[:, col:col + 1], ident[:], start=True, stop=True)
                mm.then_inc(peaks_turned, 1)

            def spread_peaks(count, n):
                pe.wait_ge(row_ready, n)
                pe.matmul(ps[:, MB, 0:count], ones[0:1, :], brow[0:1, 0:count], start=True, stop=True).then_inc(spread, 1)

            def pass1_chunk(s, c):
                for block_ in held_at.get((s, c), ()):
                    pass2_block(*block_)
                pe.wait_ge(cast_act, s * CHUNKS + c + 1)
                pe.wait_ge(cast_dve, s * CHUNKS + c + 1)
                if s == 0:
                    pe.wait_ge(x_lo, c + 1)
                elif c == 0:
                    pe.wait_ge(pass1_read, s)
                for j in range(c * GT, (c + 1) * GT):
                    for t in range(GT):
                        mm = pe.matmul(sums1[:, t, :], a8[:, s, j, t * P:(t + 1) * P], xparts[:, j, :],
                                       start=(j == 0 and t % 2 == 0), stop=(j == TILES - 1), skip_group_check=True)
                if c == CHUNKS - 1:
                    mm.then_inc(pass1_done, 1)

            def turn_x1(s):
                pe.wait_ge(x1_ready, s + 1)
                if s >= 1:
                    pe.wait_ge(rt_copied, s)
                for t in range(GT):
                    mm = pe.transpose(ps[:, MA, t * P:(t + 1) * P], rows[:, s * GT + t, :], ident[:])
                mm.then_inc(x1_turned, 1)

            def neighbour_product0(s):
                pe.wait_ge(x1t_ready, s + 1)
                for t in range(GT):
                    mm = pe.matmul(ps[:, MA, t * P:(t + 1) * P], turned[:, t * P:(t + 1) * P], wn0t_sb[:],
                                   start=True, stop=True)
                mm.then_inc(g0_done, 1)

            def self_product0(s):
                pe.wait_ge(g0_lo, s + 1)
                pe.matmul(ps[:, MA, :], ws0t_sb[:], turned[:], start=True, stop=True).then_inc(rt_done, 1)

            def pass2_block(g, jg):
                pe.wait_ge(g0_lo, jg + 1)
                first = held_first[g] == (g, jg) if g < HELD else jg == 0
                last = held_last[g] == (g, jg) if g < HELD else jg == GROUPS - 1
                for j in range(jg * GT, (jg + 1) * GT):
                    for part in range(2):
                        mm = pe.matmul(ps[:, acc_bank(g), :], gparts[:, j, part * D:(part + 1) * D], a8[:, g, j, :],
                                       start=(first and j == jg * GT and part == 0),
                                       stop=(last and j == jg * GT + GT - 1 and part == 1))
                if last:
                    mm.then_inc(pass2_done, 1)

            def small_products1(g):
                pe.wait_ge(h1_ready, g + 1)
                if g == 0:
                    pe.wait_ge(rt_copied, GROUPS)
                else:
                    pe.wait_ge(u_copied, g)
                for part, bank in enumerate((MA, MB)):
                    for t in range(GT):
                        mm = pe.matmul(ps[:, bank, t * P:(t + 1) * P], turned[:, t * P:(t + 1) * P],
                                       w1t_sb[:, part * D:(part + 1) * D], start=True, stop=True)
                mm.then_inc(g1u_done, 1)

            pe.wait_ge(consts_ready, 4)
            pe.wait_ge(w_in, 16 * 4)
            pe.wait_ge(bound_ready, 1)
            turn_peaks((0, 1), 1)
            spread_peaks(2, 1)
            for s in range(GROUPS):
                for c in range(CHUNKS):
                    pass1_chunk(s, c)
                    if s and c == C_TURN:
                        turn_x1(s - 1)
                    if s and c == C_SMALL:
                        neighbour_product0(s - 1)
                    if s and c == C_SELF:
                        self_product0(s - 1)
            ready = [b for b in held_rest if b[1] < GROUPS - 1]
            third = -(-len(ready) // 3)
            for b in ready[:third]:
                pass2_block(*b)
            turn_x1(GROUPS - 1)
            for b in ready[third:2 * third]:
                pass2_block(*b)
            neighbour_product0(GROUPS - 1)
            for b in ready[2 * third:]:
                pass2_block(*b)
            self_product0(GROUPS - 1)
            for g in range(GROUPS):
                if g < HELD:
                    pass2_block(g, GROUPS - 1)
                    if g >= 2:
                        small_products1(g - 2)
                    continue
                if g == HELD:
                    pe.wait_ge(pass1_read, GROUPS)
                else:
                    pe.wait_ge(h1_summed, g - HELD)
                for jg in range(GROUPS):
                    pass2_block(g, jg)
                    if g == HELD and jg == 0:
                        small_products1(g - 2)
                    if jg == (2 if g == HELD else 0):
                        small_products1(g - 1)
                    if g == LAST and jg == 3:
                        pe.wait_ge(g1_copied, LAST)
                        turn_peaks((2,), 2)
                    if g == LAST and jg == 4:
                        pe.wait_ge(u_copied, LAST)
                        spread_peaks(1, 2)

            def pass3_part(t, sources, part):
                for j in sources:
                    if t == 0 and j % GT == 0:
                        pe.wait_ge(g1_lo, j // GT + 1)
                    mm = pe.matmul(ps[:, P3_BANKS[t % 4], part * 2 * D:(part + 1) * 2 * D],
                                   a8[:, t // GT, j, (t % GT) * P:(t % GT + 1) * P], g1parts[:, j, :],
                                   start=(j == 0), stop=(j == sources[-1]), skip_group_check=True)
                return mm

            most, rest = range(0, LAST * GT), range(LAST * GT, TILES)
            pe.wait_ge(h1_summed, LAST)
            pass3_part(0, most, 0)
            small_products1(LAST)
            pass3_part(1, most, 0)
            pe.wait_ge(g1_copied, GROUPS)
            turn_peaks((3,), 3)
            pass3_part(2, most, 0)
            pe.wait_ge(u_copied, GROUPS)
            spread_peaks(1, 3)
            pass3_part(3, most, 0)
            for t in range(4):
                pass3_part(t, rest, 1).then_inc(pass3_done, 1)
            for t in range(4, TILES):
                pe.wait_ge(pass3_read, t - 3)
                pass3_part(t, most, 0)
                pass3_part(t, rest, 1).then_inc(pass3_done, 1)

        @block.vector
        def _(dve):
            steps = [0]

            def link(ins):
                steps[0] += 1
                ins.then_inc(dve_chain, 1)
                dve.wait_ge(dve_chain, steps[0])

            def make_scales(first, count, n):
                dve.wait_ge(peaks_turned, n)
                nc.vector.tensor_reduce(brow[0:1, 0:count], ps[0:1, MA, 0:count * P].rearrange("p (k i) -> p k i", k=count),
                                        AX.X, ALU.max).then_inc(row_ready, 1)
                dve.wait_ge(spread, n)
                cols = slice(first, first + count)
                link(nc.vector.tensor_scalar(clamped[:, cols], ps[:, MB, 0:count], 2.0 ** -36, 2.0 ** 100, ALU.max, ALU.min))
                link(nc.vector.tensor_scalar(expo[:, cols], clamped[:, cols].bitcast(I32), EXP_MASK, None, ALU.bitwise_and))
                link(nc.vector.tensor_scalar(inv[:, cols].bitcast(I32), expo[:, cols], float(SPLIT_EXP * EXP_ONE), None,
                                             ALU.subtract))
                return nc.vector.tensor_scalar(scale[:, cols].bitcast(I32), expo[:, cols], -1.0,
                                               float((2 * 127 + SPLIT_EXP) * EXP_ONE), ALU.mult, ALU.add)

            def check_range(n):
                dve.wait_ge(adj_in[n % SLOTS], 16 * (n // SLOTS + 1))
                if n:
                    dve.wait_ge(checked, n)
                v = stage[:, n % SLOTS, :].bitcast(U32)
                nc.vector.tensor_tensor_reduce(junk[:], v[:, 0:CW // 2], v[:, CW // 2:CW], 1.0, 0.0, ALU.add, ALU.max,
                                               widest[:, n:n + 1]).then_inc(checked, 1)

            def cast(n):
                g, c = divmod(n, CHUNKS)
                dve.wait_ge(adj_in[n % SLOTS], 16 * (n // SLOTS + 1))
                nc.vector.tensor_copy(a8[:, g, c * GT + ACT_TILES, :], stage[:, n % SLOTS, ACT_TILES * GW:CW],
                                      saturate=False).then_inc(cast_dve, 1)

            def norm_stats(s):
                r = rows[:, s * GT:(s + 1) * GT, :]
                dve.wait_ge(pass1_done, s + 1)
                link(nc.vector.scalar_tensor_tensor(r, r, two_sx, sums1[:, :, 0:D], ALU.mult, ALU.add))
                nc.vector.tensor_tensor(r, r, sums1[:, :, D:2 * D], ALU.add).then_inc(pass1_read, 1)
                dve.wait_ge(pass1_read, s + 1)
                for t in range(GT):
                    ins = nc.vector.bn_stats(stats[:, t, :], rows[:, s * GT + t, :])
                link(ins)
                for t in range(GT):
                    ins = nc.vector.bn_aggr(mv[:, t, :], stats[:, t, :])
                ins.then_inc(var_ready, 1)

            def newton(cols, eps, step):
                if step == 1:
                    return nc.vector.scalar_tensor_tensor(quot[:, cols], mv[:, cols, 1], eps, rstd[:, cols],
                                                          ALU.add, ALU.mult)
                if step == 2:
                    return nc.vector.scalar_tensor_tensor(std[:, cols], std2[:, cols], 0.25, quot[:, cols],
                                                          ALU.mult, ALU.add)
                return nc.vector.reciprocal(rstd[:, cols], std[:, cols])

            def normalize(s):
                dve.wait_ge(std_ready, s + 1)
                link(nc.vector.reciprocal(rstd[:], std2[:]))
                for step in (1, 2, 3):
                    link(newton(slice(0, GT), eps_sx, step))
                for t in range(GT):
                    r = rows[:, s * GT + t, :]
                    ins = nc.vector.tensor_scalar(r, r, mv[:, t, 0:1], rstd[:, t:t + 1], ALU.subtract, ALU.mult)
                ins.then_inc(x1_ready, 1)

            def split_g0_lo(s):
                dve.wait_ge(g0_hi, s + 1)
                tiles = slice(s * GT, (s + 1) * GT)
                nc.vector.scalar_tensor_tensor(gparts[:, tiles, D:2 * D], ps[:, MA, :].rearrange("p (t d) -> p t d", t=GT),
                                               scale[:, 1:2], gparts[:, tiles, 0:D], ALU.mult, ALU.subtract
                                               ).then_inc(g0_lo, 1)

            for q in range(4):
                dve.wait_ge(x_in[q], 16)
                ins = nc.vector.tensor_reduce(peaks[:, q:q + 1], rows[:, 8 * q:8 * (q + 1), :], AX.XY, ALU.max,
                                              apply_absolute_value=True)
            link(ins)
            nc.vector.tensor_reduce(bound[:, 0:1], peaks[:, 0:4], AX.X, ALU.max).then_inc(peaks_ready, 1)
            link(make_scales(0, 2, 1))
            nc.vector.tensor_scalar(two_sx, scale[:, 0:1], 2.0, None, ALU.mult)
            nc.vector.tensor_scalar(eps_sx, scale[:, 0:1], scale[:, 0:1], EPS, ALU.mult, ALU.mult)
            nc.vector.tensor_scalar(eps4_sx, scale[:, 0:1], scale[:, 0:1], 4 * EPS, ALU.mult, ALU.mult
                                    ).then_inc(scale_ready, 1)
            for n in range(SLOTS):
                cast(n)
                check_range(n)
            for s in range(GROUPS):
                for c in range(CHUNKS):
                    if s == 0:
                        dve.wait_ge(x_hi, c + 1)
                        tiles = slice(c * GT, (c + 1) * GT)
                        nc.vector.scalar_tensor_tensor(xparts[:, tiles, D:2 * D], rows[:, tiles, :], scale[:, 0:1],
                                                       xparts[:, tiles, 0:D], ALU.mult, ALU.subtract).then_inc(x_lo, 1)
                    n = s * CHUNKS + c
                    if n >= SLOTS:
                        cast(n)
                        check_range(n)
                    if s and c == C_STATS:
                        norm_stats(s - 1)
                    if s and c == C_NORM:
                        normalize(s - 1)
                    if s and c == C_SPLIT:
                        split_g0_lo(s - 1)
            norm_stats(GROUPS - 1)
            normalize(GROUPS - 1)
            split_g0_lo(GROUPS - 1)

            def sum_h1(g):
                dve.wait_ge(pass2_done, g + 1)
                dve.wait_ge(rt_copied, g + 1)
                r = rows[:, g * GT:(g + 1) * GT, :].rearrange("p t d -> p (t d)")
                nc.vector.scalar_tensor_tensor(r, ps[:, acc_bank(g), :], inv[:, 1:2], r, ALU.mult, ALU.add
                                               ).then_inc(h1_summed, 1)

            def peak_g1(g, dst):
                dve.wait_ge(g1_copied, g + 1)
                return nc.vector.tensor_reduce(dst, g1[:, g * GT:(g + 1) * GT, :], AX.XY, ALU.max,
                                               apply_absolute_value=True)

            def split_g1_lo(g, col):
                dve.wait_ge(g1_hi, g + 1)
                tiles = slice(g * GT, (g + 1) * GT)
                nc.vector.scalar_tensor_tensor(g1parts[:, tiles, D:2 * D], g1[:, tiles, :], scale[:, col:col + 1],
                                               g1parts[:, tiles, 0:D], ALU.mult, ALU.subtract).then_inc(g1_lo, 1)

            for g in range(LAST):
                sum_h1(g)
                ins = peak_g1(g, peaks[:, g:g + 1])
            link(ins)
            nc.vector.tensor_reduce(bound[:, 2:3], peaks[:, 0:LAST], AX.X, ALU.max).then_inc(peaks_ready, 1)
            make_scales(2, 1, 2).then_inc(scale_ready, 1)
            dve.wait_ge(cast_act, NCHUNK)
            for g in range(LAST):
                split_g1_lo(g, 2)
            sum_h1(LAST)
            peak_g1(LAST, bound[:, 3:4]).then_inc(peaks_ready, 1)
            make_scales(3, 1, 3).then_inc(scale_ready, 1)
            split_g1_lo(LAST, 3)
            def after(ins):
                steps[0] += 1
                ins.then_inc(dve_chain, 1)
                return steps[0]

            for t in range(TILES + 1):
                done_a = done_b = 0
                r, bank, m = rows[:, t % TILES, :], P3_BANKS[t % 4], mv[:, t % 2, :]
                last, u = t - 1, (t - 1) % 2
                for step in range(7):
                    if t < TILES:
                        if done_a:
                            dve.wait_ge(dve_chain, done_a)
                        if step == 0:
                            dve.wait_ge(pass3_done, t + 1)
                            dve.wait_ge(u_copied, t // GT + 1)
                        if step < 4:
                            col = 2 + step // 2
                            ins = nc.vector.scalar_tensor_tensor(r, ps[:, bank, step * D:(step + 1) * D],
                                                                 inv[:, col:col + 1], r, ALU.mult, ALU.add)
                            if step == 3:
                                ins.then_inc(pass3_read, 1)
                                dve.wait_ge(pass3_read, t + 1)
                            else:
                                done_a = after(ins)
                        elif step == 4:
                            dve.wait_ge(x1_back[t // (TILES // 2)], 16)
                            done_a = after(nc.vector.scalar_tensor_tensor(r, r, 0.0, g1[:, t, :], ALU.max, ALU.add))
                        elif step == 5:
                            done_a = after(nc.vector.bn_stats(stats[:, t % 2, :], r))
                        else:
                            nc.vector.bn_aggr(m, stats[:, t % 2, :]).then_inc(var3_ready, 1)
                    if t > 0:
                        if done_b:
                            dve.wait_ge(dve_chain, done_b)
                        if step == 0:
                            dve.wait_ge(std3_ready, t)
                            done_b = after(nc.vector.reciprocal(rstd[:, u:u + 1], std2[:, u:u + 1]))
                        elif step < 4:
                            done_b = after(newton(slice(u, u + 1), EPS, step))
                        elif step == 4:
                            nc.vector.tensor_scalar(rows[:, last, :], rows[:, last, :], mv[:, u, 0:1],
                                                    rstd[:, u:u + 1], ALU.subtract, ALU.mult).then_inc(out_ready, 1)


def kernel(x, adj, L1_gnn_w_self_0, L1_gnn_w_neigh_0, L1_gnn_w_self_1, L1_gnn_w_neigh_1):
    import numpy as np
    import concourse.bacc as bacc
    from concourse.bass_utils import run_bass_kernel_spmd

    adj_t = np.ascontiguousarray(
        np.asarray(adj).reshape(GROUPS, GW, CHUNKS, GT, P).transpose(0, 2, 4, 3, 1)).reshape(NCHUNK, P, CW)
    wn1_t, ws1_t = np.asarray(L1_gnn_w_neigh_1).T, np.asarray(L1_gnn_w_self_1).T
    arrays = {
        "in_x": np.ascontiguousarray(x),
        "in_adj_t": adj_t,
        "in_wn0": np.ascontiguousarray(L1_gnn_w_neigh_0),
        "in_wn0_t": np.ascontiguousarray(np.asarray(L1_gnn_w_neigh_0).T),
        "in_ws0_t": np.ascontiguousarray(np.asarray(L1_gnn_w_self_0).T),
        "in_w1_t": np.ascontiguousarray(np.concatenate([wn1_t, ws1_t], axis=1)),
    }
    nc = bacc.Bacc("TRN2", target_bir_lowering=False, num_devices=1)
    aps = [nc.dram_tensor(k, a.shape, mybir.dt.from_np(a.dtype), kind="ExternalInput").ap() for k, a in arrays.items()]
    x1_dram = nc.dram_tensor("x1_dram", (N, D), F32, kind="Internal").ap()
    out = nc.dram_tensor("out_0", (N, D), F32, kind="ExternalOutput").ap()
    graph_layers(nc, *aps, x1_dram, out)
    r = run_bass_kernel_spmd(nc, [arrays], core_ids=[0])
    return r.results[0]["out_0"]
```

```python
from contextlib import ExitStack

import concourse.bass as bass
from concourse import mybir

F32 = mybir.dt.float32
F16 = mybir.dt.float16
BF16 = mybir.dt.bfloat16
F8 = mybir.dt.float8e4
I32 = mybir.dt.int32
U32 = mybir.dt.uint32
ALU = mybir.AluOpType
ACT = mybir.ActivationFunctionType
AX = mybir.AxisListType

P = 128
N = 4096
D = 128
TILES = N // P
GT = 4
GW = GT * P
GROUPS = N // GW
CHUNKS = TILES // GT
CW = GT * GW
NCHUNK = GROUPS * CHUNKS
SLOTS = 3
HELD = 5
EARLY = 2
ACT_TILES = 3
EPS = 1e-5
F8_EXACT = 16.0
C_STATS, C_STD, C_NORM, C_TURN, C_COPY, C_SMALL, C_SPLIT, C_SELF, C_COPY_RT = 0, 1, 1, 2, 3, 4, 5, 6, 7
HELD_CHUNKS = {1: {6: 1}, 2: {0: 1, 3: 1, 6: 2}, 3: {0: 2, 3: 1, 6: 1, 7: 1}, 4: {0: 2, 3: 1, 6: 1, 7: 1},
               5: {0: 2, 3: 1, 6: 1, 7: 1}, 6: {0: 2, 3: 1, 6: 1, 7: 1}, 7: {0: 2, 3: 1, 6: 1}}
LAST = GROUPS - 1
SPLIT_EXP = 14
EXP_MASK = 0x7F800000
EXP_ONE = 1 << 23


def held_schedule():
    left = sorted(((g, j) for g in range(HELD) for j in range(GROUPS)), key=lambda b: (max(b), b[1], b[0]))
    at = {}
    for s in range(1, GROUPS):
        for c, most in HELD_CHUNKS[s].items():
            ready = [(g, j) for g, j in left
                     if (g < s or (g == s and j < c)) and (j < s - 1 or (j == s - 1 and c > C_SPLIT))]
            at[(s, c)] = ready[:most]
            left = [b for b in left if b not in at[(s, c)]]
    return at, sorted(left)


def graph_layers(nc, x, adj_t, wn0, wn0_t, ws0_t, w1_t, x1_dram, out):
    held_at, held_rest = held_schedule()
    held_first, held_last = {}, {}
    for b in [b for k in sorted(held_at) for b in held_at[k]] + held_rest:
        held_first.setdefault(b[0], b)
        held_last[b[0]] = b

    with ExitStack() as ctx:
        def sb(name, shape, dt):
            return ctx.enter_context(nc.sbuf_tensor(name, shape, dt))

        def sem(name):
            return ctx.enter_context(nc.semaphore(name))

        a8 = sb("a8", [P, GROUPS, TILES, GW], F8)
        stage = sb("stage", [P, SLOTS, CW], I32)
        xparts = sb("xparts", [P, TILES, 2 * D], F16)
        gparts = sb("gparts", [P, TILES, 2 * D], F16)
        rows = sb("rows", [P, TILES, D], F32)
        turned = sb("turned", [P, GW], F32)
        junk = sb("junk", [P, CW // 2], BF16)
        wn0t_sb = sb("wn0t_sb", [P, D], F32)
        ws0t_sb = sb("ws0t_sb", [P, D], F32)
        w1t_sb = sb("w1t_sb", [P, 2 * D], F32)
        ident = sb("ident", [P, P], F32)
        ones = sb("ones", [P, P], F32)
        peaks = sb("peaks", [P, 16], F32)
        bound = sb("bound", [P, 5], F32)
        brow = sb("brow", [P, 4], F32)
        clamped = sb("clamped", [P, 4], F32)
        expo = sb("expo", [P, 4], I32)
        scale = sb("scale", [P, 4], F32)
        inv = sb("inv", [P, 4], F32)
        cols = sb("cols", [P, 4], F32)
        two_sx = cols[:, 0:1]
        eps_sx = cols[:, 1:2]
        eps4_sx = cols[:, 2:3]
        eps4 = cols[:, 3:4]
        stats = sb("stats", [P, GT, 6], F32)
        mv = sb("mv", [P, GT, 2], F32)
        std2 = sb("std2", [P, GT], F32)
        quot = sb("quot", [P, GT], F32)
        std = sb("std", [P, GT], F32)
        rstd = sb("rstd", [P, GT], F32)
        widest = sb("widest", [P, NCHUNK], F32)
        general = sb("general", [1, 1], I32)

        ps = ctx.enter_context(nc.psum_tensor("ps", [P, 8, GW], F32))
        sums1 = ps[:, 0:2, :].rearrange("p b (t c) -> p (b t) c", t=2)
        MA, MB = 2, 1

        def acc_bank(g):
            return 3 + g if g < HELD else (0, 3, 4)[g - HELD]

        P3_BANKS = (5, 6, 7, 0)

        g1 = xparts[:].bitcast(F32)
        hidden_t = (turned[:], junk[:].bitcast(F32))
        g1parts = stage[:].rearrange("p s c -> p (s c)").bitcast(F16)[:, 0:TILES * 2 * D].rearrange(
            "p (t d) -> p t d", t=TILES)

        x_in = [sem(f"x_in{q}") for q in range(4)]
        wn0_in = sem("wn0_in")
        w_in = sem("w_in")
        adj_in = [sem(f"adj_in{k}") for k in range(SLOTS)]
        consts_ready = sem("consts_ready")
        bound_ready = sem("bound_ready")
        act_chain = sem("act_chain")
        dve_chain = sem("dve_chain")
        peaks_ready = sem("peaks_ready")
        peaks_turned = sem("peaks_turned")
        row_ready = sem("row_ready")
        spread = sem("spread")
        scale_ready = sem("scale_ready")
        x_hi = sem("x_hi")
        x_lo = sem("x_lo")
        cast_act = sem("cast_act")
        cast_dve = sem("cast_dve")
        checked = sem("checked")
        pass1_done = sem("pass1_done")
        pass1_read = sem("pass1_read")
        var_ready = sem("var_ready")
        std_ready = sem("std_ready")
        x1_ready = sem("x1_ready")
        x1_turned = sem("x1_turned")
        x1t_ready = sem("x1t_ready")
        x1_stored = sem("x1_stored")
        g0_done = sem("g0_done")
        rt_done = sem("rt_done")
        rt_copied = sem("rt_copied")
        g0_hi = sem("g0_hi")
        g0_lo = sem("g0_lo")
        pass2_done = sem("pass2_done")
        h1_summed = sem("h1_summed")
        h1_ready = sem("h1_ready")
        g1u_done = sem("g1u_done")
        g1_copied = sem("g1_copied")
        u_copied = sem("u_copied")
        g1_hi = sem("g1_hi")
        g1_lo = sem("g1_lo")
        x1_back = [sem(f"x1_back{h}") for h in range(2)]
        pass3_done = sem("pass3_done")
        pass3_read = sem("pass3_read")
        var3_ready = sem("var3_ready")
        std3_ready = sem("std3_ready")
        out_ready = sem("out_ready")
        out_stored = sem("out_stored")
        general_known = sem("general_known")
        gen_x = sem("gen_x")
        gen_in = sem("gen_in")
        gen_cast = sem("gen_cast")
        gen_mm = sem("gen_mm")
        gen_add = sem("gen_add")
        gen_chain = sem("gen_chain")
        gen_var = sem("gen_var")
        gen_std = sem("gen_std")
        gen_tile = sem("gen_tile")
        gen_turn = sem("gen_turn")
        gen_turned = sem("gen_turned")
        gen_prod = sem("gen_prod")
        gen_kept = sem("gen_kept")
        gen_out = sem("gen_out")
        gen_stored = sem("gen_stored")

        wide = a8[:].rearrange("p g t i -> p (g t i)").bitcast(F32)

        def gen_tiles(k):
            return wide[:, k * TILES * D:(k + 1) * TILES * D].rearrange("p (t d) -> p t d", t=TILES)

        gen_op, gen_sum, gen_self, gen_x1 = (gen_tiles(k) for k in range(4))
        gen_a = wide[:, 4 * TILES * D:4 * TILES * D + CW].rearrange("p (t i) -> p t i", t=GT)
        gen_t = wide[:, 4 * TILES * D + CW:4 * TILES * D + CW + D]
        gen_weights = ((wn0t_sb[:], ws0t_sb[:]), (w1t_sb[:, 0:D], w1t_sb[:, D:2 * D]))

        def tile(buffer, t):
            return buffer[:, bass.ds(t, 1), :].rearrange("p o d -> p (o d)")

        by_node = lambda t: t.rearrange("(n p) d -> p n d", p=P)
        x_nodes, x1_nodes, out_nodes = by_node(x), by_node(x1_dram), by_node(out)

        block = ctx.enter_context(nc.Block())

        @block.sync
        def _(sp):
            q = TILES // 4
            for k in range(4):
                sp.dma_start(rows[:, k * q:(k + 1) * q, :], x_nodes[:, k * q:(k + 1) * q, :]).then_inc(x_in[k], 16)
            sp.dma_start(turned[:, 0:D], wn0).then_inc(wn0_in, 16)
            for n in range(SLOTS):
                sp.dma_start(stage[:, n, :], adj_t[n]).then_inc(adj_in[n], 16)
            sp.dma_start(wn0t_sb[:], wn0_t).then_inc(w_in, 16)
            sp.dma_start(ws0t_sb[:], ws0_t).then_inc(w_in, 16)
            sp.dma_start(w1t_sb[:], w1_t).then_inc(w_in, 16)
            rounds = (NCHUNK - SLOTS) // SLOTS
            with sp.Fori(0, rounds) as r:
                for k in range(SLOTS):
                    sp.wait_ge(cast_act, r * SLOTS + (k + 1))
                    sp.wait_ge(cast_dve, r * SLOTS + (k + 1))
                    sp.wait_ge(checked, r * SLOTS + (k + 1))
                    sp.dma_start(stage[:, k, :], adj_t[bass.ds(r * SLOTS + (SLOTS + k), 1)].rearrange("o p c -> p (o c)")
                                 ).then_inc(adj_in[k], 16)
            for n in range(SLOTS + rounds * SLOTS, NCHUNK):
                sp.wait_ge(cast_act, n - SLOTS + 1)
                sp.wait_ge(cast_dve, n - SLOTS + 1)
                sp.wait_ge(checked, n - SLOTS + 1)
                sp.dma_start(stage[:, n % SLOTS, :], adj_t[n]).then_inc(adj_in[n % SLOTS], 16)
            half = TILES // 2
            for h in range(2):
                sp.wait_ge(g1_hi, GROUPS // 2 * (h + 1))
                sp.wait_ge(g1_lo, GROUPS // 2 * (h + 1))
                sp.wait_ge(x1_stored, 16 * GROUPS)
                sp.dma_start(g1[:, h * half:(h + 1) * half, :], x1_nodes[:, h * half:(h + 1) * half, :]
                             ).then_inc(x1_back[h], 16)
            stores = 0
            for t in range(TILES):
                if t % GT == GT - 1 and t < TILES - GT:
                    sp.wait_ge(out_ready, t + 1)
                    sp.dma_start(out_nodes[:, t + 1 - GT:t + 1, :], rows[:, t + 1 - GT:t + 1, :]).then_inc(out_stored, 16)
                    stores += 1
                elif t >= TILES - GT:
                    sp.wait_ge(out_ready, t + 1)
                    sp.dma_start(out_nodes[:, t:t + 1, :], rows[:, t:t + 1, :]).then_inc(out_stored, 16)
                    stores += 1
            sp.wait_ge(general_known, 1)
            needed = sp.value_load(general[0:1, 0:1], min_val=0, max_val=1)
            sp.wait_ge(out_stored, 16 * stores)
            with sp.If(needed == 1):
                sp.dma_start(gen_op, x_nodes).then_inc(gen_x, 16)
                for layer in range(3):
                    if layer:
                        sp.wait_ge(gen_cast, layer * NCHUNK)
                    sp.dma_start(stage[:, 0, :], adj_t[0]).then_inc(gen_in, 16)
                    with sp.Fori(1, NCHUNK) as n:
                        sp.wait_ge(gen_cast, n + layer * NCHUNK)
                        sp.dma_start(stage[:, 0, :], adj_t[bass.ds(n, 1)].rearrange("o p c -> p (o c)")).then_inc(gen_in, 16)
                sp.wait_ge(gen_out, TILES)
                sp.dma_start(out_nodes, gen_op).then_inc(gen_stored, 16)
                sp.wait_ge(gen_stored, 16)

        @block.gpsimd
        def _(pool):
            nc.gpsimd.memset(ident[:], 0.0).then_inc(consts_ready, 1)
            nc.gpsimd.memset(ones[:], 1.0).then_inc(consts_ready, 1)
            nc.gpsimd.memset(eps4, 4 * EPS).then_inc(consts_ready, 1)
            pool.wait_ge(consts_ready, 3)
            nc.gpsimd.affine_select(out=ident[:], in_=ident[:], compare_op=ALU.not_equal, fill=1.0, base=0,
                                    pattern=[[-1, P]], channel_multiplier=1).then_inc(consts_ready, 1)

        @block.scalar
        def _(act):
            act.wait_ge(wn0_in, 16)
            nc.scalar.activation(turned[:, D:2 * D], turned[:, 0:D], ACT.Square, accum_out=peaks[:, 15:16]).then_inc(act_chain, 1)
            act.wait_ge(act_chain, 1)
            nc.scalar.activation(bound[:, 1:2], peaks[:, 15:16], ACT.Sqrt, scale=float(D)).then_inc(bound_ready, 1)

            def cast(n):
                act.wait_ge(adj_in[n % SLOTS], 16 * (n // SLOTS + 1))
                g, c = divmod(n, CHUNKS)
                nc.scalar.activation(a8[:, g, c * GT:c * GT + ACT_TILES, :],
                                     stage[:, n % SLOTS, 0:ACT_TILES * GW].rearrange("p (t i) -> p t i", t=ACT_TILES),
                                     ACT.Copy, saturate=False).then_inc(cast_act, 1)

            def group_std(s):
                act.wait_ge(var_ready, s + 1)
                nc.scalar.activation(std2[:], mv[:, :, 1], ACT.Sqrt, bias=eps4_sx, scale=4.0).then_inc(std_ready, 1)

            def copy_x1t(s):
                act.wait_ge(x1_turned, s + 1)
                nc.scalar.activation(turned[:], ps[:, MA, :], ACT.Copy).then_inc(x1t_ready, 1)
                act.wait_ge(x1_ready, s + 1)
                act.dma_start(x1_nodes[:, s * GT:(s + 1) * GT, :], rows[:, s * GT:(s + 1) * GT, :]).then_inc(x1_stored, 16)

            def split_g0(s):
                act.wait_ge(g0_done, s + 1)
                nc.scalar.activation(gparts[:, s * GT:(s + 1) * GT, 0:D], ps[:, MA, :].rearrange("p (t d) -> p t d", t=GT),
                                     ACT.Copy, scale=scale[:, 1:2]).then_inc(g0_hi, 1)

            def copy_rt(s):
                act.wait_ge(rt_done, s + 1)
                act.wait_ge(x1_stored, 16 * (s + 1))
                nc.scalar.activation(rows[:, s * GT:(s + 1) * GT, :].rearrange("p t d -> p (t d)"), ps[:, MA, :],
                                     ACT.Copy).then_inc(rt_copied, 1)

            def split_x(c):
                nc.scalar.activation(xparts[:, c * GT:(c + 1) * GT, 0:D], rows[:, c * GT:(c + 1) * GT, :],
                                     ACT.Copy, scale=scale[:, 0:1]).then_inc(x_hi, 1)

            for n in range(EARLY):
                cast(n)
            act.wait_ge(scale_ready, 1)
            for s in range(GROUPS):
                for c in range(CHUNKS):
                    if s == 0:
                        split_x(c)
                    n = s * CHUNKS + c
                    if n >= EARLY:
                        cast(n)
                    if s:
                        if c == C_STD:
                            group_std(s - 1)
                        if c == C_COPY:
                            copy_x1t(s - 1)
                        if c == C_SPLIT:
                            split_g0(s - 1)
                        if c == C_COPY_RT:
                            copy_rt(s - 1)
            group_std(GROUPS - 1)
            copy_x1t(GROUPS - 1)
            split_g0(GROUPS - 1)
            copy_rt(GROUPS - 1)

            def relu_h1(g):
                act.wait_ge(h1_summed, g + 1)
                if g == 0:
                    act.wait_ge(rt_done, GROUPS)
                elif g == 1:
                    act.wait_ge(checked, NCHUNK)
                else:
                    act.wait_ge(g1u_done, g - 1)
                nc.scalar.activation(hidden_t[g % 2], rows[:, g * GT:(g + 1) * GT, :].rearrange("p t d -> p (t d)"),
                                     ACT.Relu).then_inc(h1_ready, 1)

            def copy_g1(g):
                act.wait_ge(g1u_done, g + 1)
                nc.scalar.activation(g1[:, g * GT:(g + 1) * GT, :], ps[:, MA, :].rearrange("p (t d) -> p t d", t=GT),
                                     ACT.Copy).then_inc(g1_copied, 1)

            def split_g1(g, col):
                act.wait_ge(g1_copied, g + 1)
                nc.scalar.activation(g1parts[:, g * GT:(g + 1) * GT, 0:D], g1[:, g * GT:(g + 1) * GT, :],
                                     ACT.Copy, scale=scale[:, col:col + 1]).then_inc(g1_hi, 1)

            relu_h1(0)
            for g in range(1, LAST):
                relu_h1(g)
                copy_g1(g - 1)
            copy_g1(LAST - 1)
            act.wait_ge(scale_ready, 2)
            act.wait_ge(checked, NCHUNK)
            act.wait_ge(cast_dve, NCHUNK)
            for g in range(LAST):
                split_g1(g, 2)
            relu_h1(LAST)
            copy_g1(LAST)
            act.wait_ge(scale_ready, 3)
            split_g1(LAST, 3)
            for t in range(TILES):
                act.wait_ge(var3_ready, t + 1)
                nc.scalar.activation(std2[:, t % 2:t % 2 + 1], mv[:, t % 2, 1:2], ACT.Sqrt, bias=eps4, scale=4.0).then_inc(std3_ready, 1)
            act.wait_ge(general_known, 1)
            needed = act.value_load(general[0:1, 0:1], min_val=0, max_val=1)
            with act.If(needed == 1):
                for layer in range(3):
                    with act.Fori(0, TILES) as t:
                        if layer != 1:
                            act.wait_ge(gen_var, t + (layer // 2 * TILES + 1))
                            nc.scalar.activation(std2[:, 0:1], mv[:, 0, 1:2], ACT.Sqrt, bias=eps4, scale=4.0
                                                 ).then_inc(gen_std, 1)
                        if layer < 2:
                            act.wait_ge(gen_turn, t + (layer * TILES + 1))
                            nc.scalar.activation(turned[:, 0:D], ps[:, MA, 0:D], ACT.Copy).then_inc(gen_turned, 1)
                            act.wait_ge(gen_prod, t + (layer * TILES + 1))
                            nc.scalar.activation(tile(gen_op, t), ps[:, MB, 0:D], ACT.Copy).then_inc(gen_kept, 1)
                            nc.scalar.activation(tile(gen_self, t), ps[:, MB, D:2 * D], ACT.Copy).then_inc(gen_kept, 1)

        @block.tensor
        def _(pe):
            def turn_peaks(cols, n):
                pe.wait_ge(peaks_ready, n)
                for k, col in enumerate(cols):
                    mm = pe.matmul(ps[0:1, MA, k * P:(k + 1) * P], bound[:, col:col + 1], ident[:], start=True, stop=True)
                mm.then_inc(peaks_turned, 1)

            def spread_peaks(count, n):
                pe.wait_ge(row_ready, n)
                pe.matmul(ps[:, MB, 0:count], ones[0:1, :], brow[0:1, 0:count], start=True, stop=True).then_inc(spread, 1)

            def pass1_chunk(s, c):
                for block_ in held_at.get((s, c), ()):
                    pass2_block(*block_)
                pe.wait_ge(cast_act, s * CHUNKS + c + 1)
                pe.wait_ge(cast_dve, s * CHUNKS + c + 1)
                if s == 0:
                    pe.wait_ge(x_lo, c + 1)
                elif c == 0:
                    pe.wait_ge(pass1_read, s)
                for j in range(c * GT, (c + 1) * GT):
                    for t in range(GT):
                        mm = pe.matmul(sums1[:, t, :], a8[:, s, j, t * P:(t + 1) * P], xparts[:, j, :],
                                       start=(j == 0 and t % 2 == 0), stop=(j == TILES - 1), skip_group_check=True)
                if c == CHUNKS - 1:
                    mm.then_inc(pass1_done, 1)

            def turn_x1(s):
                pe.wait_ge(x1_ready, s + 1)
                if s >= 1:
                    pe.wait_ge(rt_copied, s)
                for t in range(GT):
                    mm = pe.transpose(ps[:, MA, t * P:(t + 1) * P], rows[:, s * GT + t, :], ident[:])
                mm.then_inc(x1_turned, 1)

            def neighbour_product0(s):
                pe.wait_ge(x1t_ready, s + 1)
                if s == 0:
                    pe.wait_ge(w_in, 16 * 3)
                for t in range(GT):
                    mm = pe.matmul(ps[:, MA, t * P:(t + 1) * P], turned[:, t * P:(t + 1) * P], wn0t_sb[:],
                                   start=True, stop=True)
                mm.then_inc(g0_done, 1)

            def self_product0(s):
                pe.wait_ge(g0_lo, s + 1)
                pe.matmul(ps[:, MA, :], ws0t_sb[:], turned[:], start=True, stop=True).then_inc(rt_done, 1)

            def pass2_block(g, jg):
                pe.wait_ge(g0_lo, jg + 1)
                first = held_first[g] == (g, jg) if g < HELD else jg == 0
                last = held_last[g] == (g, jg) if g < HELD else jg == GROUPS - 1
                for j in range(jg * GT, (jg + 1) * GT):
                    for part in range(2):
                        mm = pe.matmul(ps[:, acc_bank(g), :], gparts[:, j, part * D:(part + 1) * D], a8[:, g, j, :],
                                       start=(first and j == jg * GT and part == 0),
                                       stop=(last and j == jg * GT + GT - 1 and part == 1))
                if last:
                    mm.then_inc(pass2_done, 1)

            def small_products1(g):
                pe.wait_ge(h1_ready, g + 1)
                if g == 0:
                    pe.wait_ge(rt_copied, GROUPS)
                else:
                    pe.wait_ge(g1_copied, g)
                    pe.wait_ge(u_copied, g)
                for part, bank in enumerate((MA, MB)):
                    for t in range(GT):
                        mm = pe.matmul(ps[:, bank, t * P:(t + 1) * P], hidden_t[g % 2][:, t * P:(t + 1) * P],
                                       w1t_sb[:, part * D:(part + 1) * D], start=True, stop=True)
                mm.then_inc(g1u_done, 1)

            pe.wait_ge(consts_ready, 4)
            pe.wait_ge(bound_ready, 1)
            turn_peaks((0, 1), 1)
            spread_peaks(2, 1)
            for s in range(GROUPS):
                for c in range(CHUNKS):
                    pass1_chunk(s, c)
                    if s and c == C_TURN:
                        turn_x1(s - 1)
                    if s and c == C_SMALL:
                        neighbour_product0(s - 1)
                    if s and c == C_SELF:
                        self_product0(s - 1)
            ready = [b for b in held_rest if b[1] < GROUPS - 1]
            third = -(-len(ready) // 3)
            for b in ready[:third]:
                pass2_block(*b)
            turn_x1(GROUPS - 1)
            for b in ready[third:2 * third]:
                pass2_block(*b)
            neighbour_product0(GROUPS - 1)
            for b in ready[2 * third:]:
                pass2_block(*b)
            self_product0(GROUPS - 1)
            for g in range(GROUPS):
                if g < HELD:
                    pass2_block(g, GROUPS - 1)
                    if g >= 2:
                        small_products1(g - 2)
                    continue
                if g == HELD:
                    pe.wait_ge(pass1_read, GROUPS)
                else:
                    pe.wait_ge(h1_summed, g - HELD)
                for jg in range(GROUPS):
                    pass2_block(g, jg)
                    if g == HELD and jg == 0:
                        small_products1(g - 2)
                    if jg == (2 if g == HELD else 0):
                        small_products1(g - 1)
                    if g == LAST and jg == 3:
                        pe.wait_ge(g1_copied, LAST)
                        turn_peaks((2, 4), 3)
                    if g == LAST and jg == 4:
                        pe.wait_ge(u_copied, LAST)
                        spread_peaks(1, 2)

            def pass3_part(t, sources, part):
                for j in sources:
                    if t == 0 and j % GT == 0:
                        pe.wait_ge(g1_lo, j // GT + 1)
                    mm = pe.matmul(ps[:, P3_BANKS[t % 4], part * 2 * D:(part + 1) * 2 * D],
                                   a8[:, t // GT, j, (t % GT) * P:(t % GT + 1) * P], g1parts[:, j, :],
                                   start=(j == 0), stop=(j == sources[-1]), skip_group_check=True)
                return mm

            most, rest = range(0, LAST * GT), range(LAST * GT, TILES)
            pe.wait_ge(h1_summed, LAST)
            pass3_part(0, most, 0)
            small_products1(LAST)
            pass3_part(1, most, 0)
            pe.wait_ge(g1_copied, GROUPS)
            turn_peaks((3,), 4)
            pass3_part(2, most, 0)
            pe.wait_ge(u_copied, GROUPS)
            spread_peaks(1, 3)
            pass3_part(3, most, 0)
            for t in range(4):
                pass3_part(t, rest, 1).then_inc(pass3_done, 1)
            for t in range(4, TILES):
                pe.wait_ge(pass3_read, t - 3)
                pass3_part(t, most, 0)
                pass3_part(t, rest, 1).then_inc(pass3_done, 1)

            pe.wait_ge(general_known, 1)
            needed = pe.value_load(general[0:1, 0:1], min_val=0, max_val=1)
            with pe.If(needed == 1):
                pe.wait_ge(gen_x, 16)
                for layer in range(3):
                    with pe.Fori(0, GROUPS) as g:
                        with pe.Fori(0, CHUNKS) as c:
                            pe.wait_ge(gen_cast, g * CHUNKS + c + (layer * NCHUNK + 1))
                            for k in range(GT):
                                for t in range(GT):
                                    mm = pe.matmul(ps[:, GT + t, 0:D], gen_a[:, k, t * P:(t + 1) * P],
                                                   tile(gen_op, c * GT + k), start=(k == 0), stop=(k == GT - 1))
                            mm.then_inc(gen_mm, 1)
                    if layer < 2:
                        with pe.Fori(0, TILES) as t:
                            pe.wait_ge(gen_tile, t + (layer * TILES + 1))
                            pe.transpose(ps[:, MA, 0:D], gen_t, ident[:]).then_inc(gen_turn, 1)
                            pe.wait_ge(gen_turned, t + (layer * TILES + 1))
                            for k in range(2):
                                mm = pe.matmul(ps[:, MB, k * D:(k + 1) * D], turned[:, 0:D], gen_weights[layer][k],
                                               start=True, stop=True)
                            mm.then_inc(gen_prod, 1)

        @block.vector
        def _(dve):
            steps = [0]

            def link(ins):
                steps[0] += 1
                ins.then_inc(dve_chain, 1)
                dve.wait_ge(dve_chain, steps[0])

            def make_scales(first, count, n, extra=0):
                dve.wait_ge(peaks_turned, n)
                taken = count + extra
                nc.vector.tensor_reduce(brow[0:1, 0:taken], ps[0:1, MA, 0:taken * P].rearrange("p (k i) -> p k i", k=taken),
                                        AX.X, ALU.max).then_inc(row_ready, 1)
                dve.wait_ge(spread, n)
                cols = slice(first, first + count)
                link(nc.vector.tensor_scalar(clamped[:, cols], ps[:, MB, 0:count], 2.0 ** -36, 2.0 ** 100, ALU.max, ALU.min))
                link(nc.vector.tensor_scalar(expo[:, cols], clamped[:, cols].bitcast(I32), EXP_MASK, None, ALU.bitwise_and))
                link(nc.vector.tensor_scalar(inv[:, cols].bitcast(I32), expo[:, cols], float(SPLIT_EXP * EXP_ONE), None,
                                             ALU.subtract))
                return nc.vector.tensor_scalar(scale[:, cols].bitcast(I32), expo[:, cols], -1.0,
                                               float((2 * 127 + SPLIT_EXP) * EXP_ONE), ALU.mult, ALU.add)

            def check_range(n):
                dve.wait_ge(adj_in[n % SLOTS], 16 * (n // SLOTS + 1))
                if n:
                    dve.wait_ge(checked, n)
                v = stage[:, n % SLOTS, :].bitcast(U32)
                nc.vector.tensor_tensor_reduce(junk[:], v[:, 0:CW // 2], v[:, CW // 2:CW], 1.0, 0.0, ALU.add, ALU.max,
                                               widest[:, n:n + 1]).then_inc(checked, 1)

            def cast(n):
                g, c = divmod(n, CHUNKS)
                dve.wait_ge(adj_in[n % SLOTS], 16 * (n // SLOTS + 1))
                nc.vector.tensor_copy(a8[:, g, c * GT + ACT_TILES, :], stage[:, n % SLOTS, ACT_TILES * GW:CW],
                                      saturate=False).then_inc(cast_dve, 1)

            def norm_stats(s):
                r = rows[:, s * GT:(s + 1) * GT, :]
                dve.wait_ge(pass1_done, s + 1)
                link(nc.vector.scalar_tensor_tensor(r, r, two_sx, sums1[:, :, 0:D], ALU.mult, ALU.add))
                nc.vector.tensor_tensor(r, r, sums1[:, :, D:2 * D], ALU.add).then_inc(pass1_read, 1)
                dve.wait_ge(pass1_read, s + 1)
                for t in range(GT):
                    ins = nc.vector.bn_stats(stats[:, t, :], rows[:, s * GT + t, :])
                link(ins)
                for t in range(GT):
                    ins = nc.vector.bn_aggr(mv[:, t, :], stats[:, t, :])
                ins.then_inc(var_ready, 1)

            def newton(cols, eps, step):
                if step == 1:
                    return nc.vector.scalar_tensor_tensor(quot[:, cols], mv[:, cols, 1], eps, rstd[:, cols],
                                                          ALU.add, ALU.mult)
                if step == 2:
                    return nc.vector.scalar_tensor_tensor(std[:, cols], std2[:, cols], 0.25, quot[:, cols],
                                                          ALU.mult, ALU.add)
                return nc.vector.reciprocal(rstd[:, cols], std[:, cols])

            def normalize(s):
                dve.wait_ge(std_ready, s + 1)
                link(nc.vector.reciprocal(rstd[:], std2[:]))
                for step in (1, 2, 3):
                    link(newton(slice(0, GT), eps_sx, step))
                for t in range(GT):
                    r = rows[:, s * GT + t, :]
                    ins = nc.vector.tensor_scalar(r, r, mv[:, t, 0:1], rstd[:, t:t + 1], ALU.subtract, ALU.mult)
                ins.then_inc(x1_ready, 1)

            def split_g0_lo(s):
                dve.wait_ge(g0_hi, s + 1)
                tiles = slice(s * GT, (s + 1) * GT)
                nc.vector.scalar_tensor_tensor(gparts[:, tiles, D:2 * D], ps[:, MA, :].rearrange("p (t d) -> p t d", t=GT),
                                               scale[:, 1:2], gparts[:, tiles, 0:D], ALU.mult, ALU.subtract
                                               ).then_inc(g0_lo, 1)

            for q in range(4):
                dve.wait_ge(x_in[q], 16)
                ins = nc.vector.tensor_reduce(peaks[:, q:q + 1], rows[:, 8 * q:8 * (q + 1), :], AX.XY, ALU.max,
                                              apply_absolute_value=True)
            link(ins)
            nc.vector.tensor_reduce(bound[:, 0:1], peaks[:, 0:4], AX.X, ALU.max).then_inc(peaks_ready, 1)
            link(make_scales(0, 2, 1))
            nc.vector.tensor_scalar(two_sx, scale[:, 0:1], 2.0, None, ALU.mult)
            nc.vector.tensor_scalar(eps_sx, scale[:, 0:1], scale[:, 0:1], EPS, ALU.mult, ALU.mult)
            nc.vector.tensor_scalar(eps4_sx, scale[:, 0:1], scale[:, 0:1], 4 * EPS, ALU.mult, ALU.mult
                                    ).then_inc(scale_ready, 1)
            for n in range(EARLY):
                cast(n)
                check_range(n)
            for s in range(GROUPS):
                for c in range(CHUNKS):
                    if s == 0:
                        dve.wait_ge(x_hi, c + 1)
                        tiles = slice(c * GT, (c + 1) * GT)
                        nc.vector.scalar_tensor_tensor(xparts[:, tiles, D:2 * D], rows[:, tiles, :], scale[:, 0:1],
                                                       xparts[:, tiles, 0:D], ALU.mult, ALU.subtract).then_inc(x_lo, 1)
                    n = s * CHUNKS + c
                    if n >= EARLY:
                        cast(n)
                        check_range(n)
                    if s and c == C_STATS:
                        norm_stats(s - 1)
                    if s and c == C_NORM:
                        normalize(s - 1)
                    if s and c == C_SPLIT:
                        split_g0_lo(s - 1)
            norm_stats(GROUPS - 1)
            normalize(GROUPS - 1)
            split_g0_lo(GROUPS - 1)

            def sum_h1(g):
                dve.wait_ge(pass2_done, g + 1)
                dve.wait_ge(rt_copied, g + 1)
                r = rows[:, g * GT:(g + 1) * GT, :].rearrange("p t d -> p (t d)")
                nc.vector.scalar_tensor_tensor(r, ps[:, acc_bank(g), :], inv[:, 1:2], r, ALU.mult, ALU.add
                                               ).then_inc(h1_summed, 1)

            def peak_g1(g, dst):
                dve.wait_ge(g1_copied, g + 1)
                return nc.vector.tensor_reduce(dst, g1[:, g * GT:(g + 1) * GT, :], AX.XY, ALU.max,
                                               apply_absolute_value=True)

            def split_g1_lo(g, col):
                dve.wait_ge(g1_hi, g + 1)
                tiles = slice(g * GT, (g + 1) * GT)
                nc.vector.scalar_tensor_tensor(g1parts[:, tiles, D:2 * D], g1[:, tiles, :], scale[:, col:col + 1],
                                               g1parts[:, tiles, 0:D], ALU.mult, ALU.subtract).then_inc(g1_lo, 1)

            def copy_u(g):
                dve.wait_ge(g1u_done, g + 1)
                nc.vector.tensor_copy(rows[:, g * GT:(g + 1) * GT, :], ps[:, MB, :].rearrange("p (t d) -> p t d", t=GT)
                                      ).then_inc(u_copied, 1)

            sum_h1(0)
            for g in range(LAST):
                if g + 1 < LAST:
                    sum_h1(g + 1)
                copy_u(g)
                ins = peak_g1(g, peaks[:, g:g + 1])
            link(ins)
            nc.vector.tensor_reduce(bound[:, 2:3], peaks[:, 0:LAST], AX.X, ALU.max).then_inc(peaks_ready, 1)
            dve.wait_ge(checked, NCHUNK)
            nc.vector.tensor_reduce(bound[:, 4:5], widest[:], AX.X, ALU.max).then_inc(peaks_ready, 1)
            make_scales(2, 1, 2, extra=1).then_inc(scale_ready, 1)
            nc.vector.tensor_scalar(general[:], brow[0:1, 1:2], F8_EXACT, None, ALU.is_gt).then_inc(general_known, 1)
            dve.wait_ge(cast_act, NCHUNK)
            for g in range(LAST):
                split_g1_lo(g, 2)
            sum_h1(LAST)
            copy_u(LAST)
            peak_g1(LAST, bound[:, 3:4]).then_inc(peaks_ready, 1)
            make_scales(3, 1, 3).then_inc(scale_ready, 1)
            split_g1_lo(LAST, 3)
            def after(ins):
                steps[0] += 1
                ins.then_inc(dve_chain, 1)
                return steps[0]

            for t in range(TILES + 1):
                done_a = done_b = 0
                r, bank, m = rows[:, t % TILES, :], P3_BANKS[t % 4], mv[:, t % 2, :]
                last, u = t - 1, (t - 1) % 2
                for step in range(7):
                    if t < TILES:
                        if done_a:
                            dve.wait_ge(dve_chain, done_a)
                        if step == 0:
                            dve.wait_ge(pass3_done, t + 1)
                            dve.wait_ge(u_copied, t // GT + 1)
                        if step < 4:
                            col = 2 + step // 2
                            ins = nc.vector.scalar_tensor_tensor(r, ps[:, bank, step * D:(step + 1) * D],
                                                                 inv[:, col:col + 1], r, ALU.mult, ALU.add)
                            if step == 3:
                                ins.then_inc(pass3_read, 1)
                                dve.wait_ge(pass3_read, t + 1)
                            else:
                                done_a = after(ins)
                        elif step == 4:
                            dve.wait_ge(x1_back[t // (TILES // 2)], 16)
                            done_a = after(nc.vector.scalar_tensor_tensor(r, r, 0.0, g1[:, t, :], ALU.max, ALU.add))
                        elif step == 5:
                            done_a = after(nc.vector.bn_stats(stats[:, t % 2, :], r))
                        else:
                            nc.vector.bn_aggr(m, stats[:, t % 2, :]).then_inc(var3_ready, 1)
                    if t > 0:
                        if done_b:
                            dve.wait_ge(dve_chain, done_b)
                        if step == 0:
                            dve.wait_ge(std3_ready, t)
                            done_b = after(nc.vector.reciprocal(rstd[:, u:u + 1], std2[:, u:u + 1]))
                        elif step < 4:
                            done_b = after(newton(slice(u, u + 1), EPS, step))
                        elif step == 4:
                            nc.vector.tensor_scalar(rows[:, last, :], rows[:, last, :], mv[:, u, 0:1],
                                                    rstd[:, u:u + 1], ALU.subtract, ALU.mult).then_inc(out_ready, 1)


            dve.wait_ge(general_known, 1)
            needed = dve.value_load(general[0:1, 0:1], min_val=0, max_val=1)
            with dve.If(needed == 1):
                one = slice(0, 1)
                links = [0]

                def gen_sums(layer):
                    nc.vector.memset(gen_sum, 0.0).then_inc(gen_chain, 1)
                    links[0] += 1
                    dve.wait_ge(gen_chain, links[0])
                    with dve.Fori(0, GROUPS) as g:
                        with dve.Fori(0, CHUNKS) as c:
                            n = g * CHUNKS + c + (layer * NCHUNK + 1)
                            dve.wait_ge(gen_in, n * 16)
                            nc.vector.tensor_copy(gen_a, stage[:, 0, :].rearrange("p (t i) -> p t i", t=GT)
                                                  ).then_inc(gen_cast, 1)
                            dve.wait_ge(gen_mm, n)
                            sums = gen_sum[:, bass.ds(g * GT, GT), :]
                            nc.vector.tensor_tensor(sums, ps[:, GT:2 * GT, 0:D], sums, ALU.add).then_inc(gen_add, 1)
                            dve.wait_ge(gen_add, n)

                def gen_step(ins, t, per_tile, k):
                    ins.then_inc(gen_chain, 1)
                    dve.wait_ge(gen_chain, t * per_tile + (links[0] + k))

                def gen_norm(t, per_tile, k, normed, result):
                    gen_step(nc.vector.bn_stats(stats[:, 0, :], gen_t), t, per_tile, k)
                    nc.vector.memset(quot[:, one], 0.0)
                    nc.vector.bn_aggr(mv[:, 0, :], stats[:, 0, :]).then_inc(gen_var, 1)
                    dve.wait_ge(gen_std, t + (normed + 1))
                    gen_step(nc.vector.reciprocal(rstd[:, one], std2[:, one]), t, per_tile, k + 1)
                    for step in (1, 2, 3):
                        gen_step(newton(one, EPS, step), t, per_tile, k + 1 + step)
                    return nc.vector.tensor_scalar(result, gen_t, mv[:, 0, 0:1], rstd[:, 0:1], ALU.subtract, ALU.mult)

                dve.wait_ge(gen_x, 16)
                gen_sums(0)
                per_tile = 6
                with dve.Fori(0, TILES) as t:
                    gen_step(nc.vector.scalar_tensor_tensor(gen_t, tile(gen_op, t), 2.0, tile(gen_sum, t),
                                                            ALU.mult, ALU.add), t, per_tile, 1)
                    gen_norm(t, per_tile, 2, 0, tile(gen_x1, t))
                    nc.vector.tensor_scalar(gen_t, gen_t, mv[:, 0, 0:1], rstd[:, 0:1], ALU.subtract, ALU.mult
                                            ).then_inc(gen_tile, 1)
                    dve.wait_ge(gen_kept, t * 2 + 2)
                links[0] += per_tile * TILES
                gen_sums(1)
                per_tile = 1
                with dve.Fori(0, TILES) as t:
                    gen_step(nc.vector.tensor_tensor(gen_t, tile(gen_self, t), tile(gen_sum, t), ALU.add), t, per_tile, 1)
                    nc.vector.tensor_scalar(gen_t, gen_t, 0.0, None, ALU.max).then_inc(gen_tile, 1)
                    dve.wait_ge(gen_kept, t * 2 + (TILES * 2 + 2))
                links[0] += per_tile * TILES
                gen_sums(2)
                per_tile = 7
                with dve.Fori(0, TILES) as t:
                    gen_step(nc.vector.tensor_tensor(gen_t, tile(gen_self, t), tile(gen_sum, t), ALU.add), t, per_tile, 1)
                    gen_step(nc.vector.scalar_tensor_tensor(gen_t, gen_t, 0.0, tile(gen_x1, t), ALU.max, ALU.add),
                             t, per_tile, 2)
                    gen_norm(t, per_tile, 3, TILES, tile(gen_op, t)).then_inc(gen_out, 1)
                    dve.wait_ge(gen_out, t + 1)


def kernel(x, adj, L1_gnn_w_self_0, L1_gnn_w_neigh_0, L1_gnn_w_self_1, L1_gnn_w_neigh_1):
    import numpy as np
    import concourse.bacc as bacc
    from concourse.bass_utils import run_bass_kernel_spmd

    adj_t = np.ascontiguousarray(
        np.asarray(adj).reshape(GROUPS, GW, CHUNKS, GT, P).transpose(0, 2, 4, 3, 1)).reshape(NCHUNK, P, CW)
    wn1_t, ws1_t = np.asarray(L1_gnn_w_neigh_1).T, np.asarray(L1_gnn_w_self_1).T
    arrays = {
        "in_x": np.ascontiguousarray(x),
        "in_adj_t": adj_t,
        "in_wn0": np.ascontiguousarray(L1_gnn_w_neigh_0),
        "in_wn0_t": np.ascontiguousarray(np.asarray(L1_gnn_w_neigh_0).T),
        "in_ws0_t": np.ascontiguousarray(np.asarray(L1_gnn_w_self_0).T),
        "in_w1_t": np.ascontiguousarray(np.concatenate([wn1_t, ws1_t], axis=1)),
    }
    nc = bacc.Bacc("TRN2", target_bir_lowering=False, num_devices=1)
    aps = [nc.dram_tensor(k, a.shape, mybir.dt.from_np(a.dtype), kind="ExternalInput").ap() for k, a in arrays.items()]
    x1_dram = nc.dram_tensor("x1_dram", (N, D), F32, kind="Internal").ap()
    out = nc.dram_tensor("out_0", (N, D), F32, kind="ExternalOutput").ap()
    graph_layers(nc, *aps, x1_dram, out)
    r = run_bass_kernel_spmd(nc, [arrays], core_ids=[0])
    return r.results[0]["out_0"]
```
